# Optimizing a Trainium2 kernel written in Bass

```python
import numpy as np
import jax
import jax.numpy as jnp

def _softmax(x, axis=-1):
    return jax.nn.softmax(x, axis=axis)

def _gelu(x):
    return jax.nn.gelu(x, approximate=True)

def _silu(x):
    return jax.nn.silu(x)

def _sigmoid(x):
    return jax.nn.sigmoid(x)

def _layernorm(x, axis=-1, eps=1e-05):
    m = jnp.mean(x, axis=axis, keepdims=True)
    v = jnp.var(x, axis=axis, keepdims=True)
    return (x - m) / jnp.sqrt(v + eps)

def _scatter_add(tgt, idx, src, axis=0):
    return tgt.at[idx].add(src)

def _segment_sum(src, seg, n):
    return jax.ops.segment_sum(src, seg, n)
kernel_name = 'mk_flamingo_gated_d1_seqx_r8_16f9f3'

def setup_inputs(seed: int=0):
    np.random.seed(seed)
    _w = jnp.asarray

    def _rec_inputs():
        import jax
        import jax.numpy as jnp
        _rk = jax.random.key(seed)
        x = 7.22e-05 + 1 * jax.random.normal(jax.random.fold_in(_rk, 1), (8, 128, 512), jnp.float32)
        _lenS = 128 - jax.random.randint(jax.random.fold_in(_rk, 7), (8,), 0, max(1, 128 // 4) + 1, jnp.int32)
        _lenS2 = 128 - jax.random.randint(jax.random.fold_in(_rk, 8), (8,), 0, max(1, 128 // 4) + 1, jnp.int32)
        _ctx_4096P = jax.random.normal(jax.random.fold_in(_rk, 11), (8, 16, 512), jnp.float32)
        _ctx_4096c = jax.random.dirichlet(jax.random.fold_in(_rk, 511), 0.3 * jnp.ones((16,), jnp.float32), (8, 128))
        _ctx_4096t = jnp.einsum('bsk,bkd->bsd', _ctx_4096c, _ctx_4096P)
        _ctx_4096t = _ctx_4096t * jax.lax.rsqrt(jnp.mean(jnp.square(_ctx_4096t)) + 1e-12) * 0.953939
        ctx_4096 = 4.13588e-05 + 0.999923 * (_ctx_4096t + 0.3 * jax.random.normal(jax.random.fold_in(_rk, 611), (8, 128, 512), jnp.float32))
        _validS = jnp.arange(128)[None, :] < _lenS[:, None]
        _validS2 = jnp.arange(128)[None, :] < _lenS2[:, None]
        _causal = jnp.tril(jnp.ones((128, 128), dtype=bool))
        mask_BxSxS2_bk0 = jnp.logical_not(jnp.broadcast_to(_validS2[:, None, :], (8, 128, 128)))
        _g = jax.random.normal(jax.random.fold_in(_rk, 9001), (2, 1), jnp.float32)
        _g = jnp.sign(_g) * jnp.maximum(jnp.abs(_g), 1.0) + (_g == 0) * 1.0
        g_xattn = _g[0]
        g_ffn = _g[1]
        return (x, ctx_4096, mask_BxSxS2_bk0, g_xattn, g_ffn)
    x, ctx_4096, mask_BxSxS2_bk0, g_xattn, g_ffn = _rec_inputs()

    def _L0_xattn_setup():
        import jax, jax.numpy as jnp
        import numpy as np
        B, LQ, LK, D, H, DH = (2, 128, 128, 512, 32, 128)
        EPS = 1e-05

        def _rmsnorm(x, weight):
            var = jnp.mean(jnp.square(x), axis=-1, keepdims=True)
            return x * jax.lax.rsqrt(var + EPS) * weight
        key = jax.random.key(seed)
        ks = jax.random.split(key, 8)
        scale = 0.02
        return {'hidden_states': jax.random.normal(ks[0], (B, LQ, D), jnp.float32), 'key_value_states': jax.random.normal(ks[1], (B, LK, D), jnp.float32), 'attention_mask': jax.random.randint(ks[2], (B, LQ, LK), 0, 2) > 0, 'position_bias': jax.random.normal(ks[3], (H, LQ, LK), jnp.float32), 'ln_weight': jnp.ones((D,), jnp.float32), 'w_q': jax.random.normal(ks[4], (H * DH, D), jnp.float32) * scale, 'w_k': jax.random.normal(ks[5], (H * DH, D), jnp.float32) * scale, 'w_v': jax.random.normal(ks[6], (H * DH, D), jnp.float32) * scale, 'w_out': jax.random.normal(ks[7], (D, H * DH), jnp.float32) * scale}
    _L0_xattn_all = _L0_xattn_setup()
    _L0_xattn_in = {k: v for k, v in _L0_xattn_all.items() if k in ('position_bias', 'ln_weight', 'w_q', 'w_k', 'w_v', 'w_out')}
    del _L0_xattn_all

    def _L0_ffn_setup():
        import jax, jax.numpy as jnp
        import numpy as np

        def _simulate_fp8_e4m3(w):
            return w.astype(jnp.float8_e4m3fn).astype(jnp.float32)
        key = jax.random.key(seed)
        k_x, k_w, k_s, k_b = jax.random.split(key, 4)
        B, S, D_in, D_out = (4, 256, 512, 512)
        x = jax.random.normal(k_x, (B, S, D_in), dtype=jnp.bfloat16)
        w_real = jax.random.normal(k_w, (D_out, D_in), dtype=jnp.float32) * 0.02
        weight_scale = jnp.array([0.001], dtype=jnp.float32)
        weight = _simulate_fp8_e4m3(w_real / weight_scale)
        bias = jax.random.normal(k_b, (D_out,), dtype=jnp.float32) * 0.02
        return {'x': x, 'weight': weight, 'weight_scale': weight_scale, 'bias': bias}
    _L0_ffn_all = _L0_ffn_setup()
    _L0_ffn_in = {k: v for k, v in _L0_ffn_all.items() if k in ('weight', 'weight_scale', 'bias')}
    del _L0_ffn_all
    return {'x': x, 'ctx_4096': ctx_4096, 'mask_BxSxS2_bk0': mask_BxSxS2_bk0, 'g_xattn': g_xattn, 'g_ffn': g_ffn, 'L0_xattn_position_bias': _L0_xattn_in['position_bias'], 'L0_xattn_ln_weight': _L0_xattn_in['ln_weight'], 'L0_xattn_w_q': _L0_xattn_in['w_q'], 'L0_xattn_w_k': _L0_xattn_in['w_k'], 'L0_xattn_w_v': _L0_xattn_in['w_v'], 'L0_xattn_w_out': _L0_xattn_in['w_out'], 'L0_ffn_weight': _L0_ffn_in['weight'], 'L0_ffn_weight_scale': _L0_ffn_in['weight_scale'], 'L0_ffn_bias': _L0_ffn_in['bias']}

def reference(x, ctx_4096, mask_BxSxS2_bk0, g_xattn, g_ffn, L0_xattn_position_bias, L0_xattn_ln_weight, L0_xattn_w_q, L0_xattn_w_k, L0_xattn_w_v, L0_xattn_w_out, L0_ffn_weight, L0_ffn_weight_scale, L0_ffn_bias):
    import jax
    import jax.numpy as jnp

    def _L0_xattn_ref(hidden_states, key_value_states, attention_mask, position_bias, ln_weight, w_q, w_k, w_v, w_out):
        import jax, jax.numpy as jnp
        import numpy as np
        B, LQ, LK, D, H, DH = (2, 128, 128, 512, 32, 128)
        EPS = 1e-05

        def _rmsnorm(x, weight):
            var = jnp.mean(jnp.square(x), axis=-1, keepdims=True)
            return x * jax.lax.rsqrt(var + EPS) * weight
        x = _rmsnorm(hidden_states, ln_weight)
        b, lq, _ = x.shape
        lk = key_value_states.shape[1]
        h_q = (x @ w_q.T).reshape(b, lq, H, DH)
        h_k = (key_value_states @ w_k.T).reshape(b, lk, H, DH)
        h_v = (key_value_states @ w_v.T).reshape(b, lk, H, DH)
        score = jnp.einsum('bqhd,bkhd->bhqk', h_q, h_k)
        score = score + position_bias[None]
        m = attention_mask[:, None]
        score = jnp.where(m, score, -jnp.inf)
        score = jax.nn.softmax(score, axis=-1)
        score = jnp.where(m, score, 0.0)
        attn = jnp.einsum('bhqk,bkhd->bqhd', score, h_v).reshape(b, lq, H * DH)
        out = attn @ w_out.T
        return hidden_states + out

    def _L0_ffn_ref(x, weight, weight_scale, bias):
        import jax, jax.numpy as jnp
        import numpy as np

        def _simulate_fp8_e4m3(w):
            return w.astype(jnp.float8_e4m3fn).astype(jnp.float32)
        out_dtype = x.dtype
        w_deq = (weight * weight_scale).astype(out_dtype)
        out = jnp.einsum('bsi,oi->bso', x, w_deq)
        out = out + bias.astype(out_dtype)
        return out.astype(out_dtype)
    x = x + jnp.tanh(g_xattn[0]) * _L0_xattn_ref(_layernorm(x, axis=-1), ctx_4096, mask_BxSxS2_bk0, L0_xattn_position_bias, L0_xattn_ln_weight, L0_xattn_w_q, L0_xattn_w_k, L0_xattn_w_v, L0_xattn_w_out)
    x = x + jnp.tanh(g_ffn[0]) * _L0_ffn_ref(_layernorm(x, axis=-1), L0_ffn_weight, L0_ffn_weight_scale, L0_ffn_bias)
    return x

_drawn_inputs = setup_inputs


def setup_inputs(seed=0):
    import zlib

    import numpy as np

    out = dict(_drawn_inputs(seed))
    spreads = {'L0_xattn_ln_weight': (1.0, 0.544)}
    factors = {'L0_ffn_bias': 5.963}
    for name, (base, spread) in spreads.items():
        noise = np.random.default_rng([zlib.crc32(name.encode()), seed]).standard_normal(out[name].shape)
        drawn = base * np.exp(spread * noise) if base else spread * noise
        out[name] = jnp.asarray(drawn.astype(out[name].dtype))
    for name, factor in factors.items():
        out[name] = (out[name] * factor).astype(out[name].dtype)
    return out
```

```python
from contextlib import ExitStack

import concourse.bass as bass
from concourse import mybir

ALU = mybir.AluOpType
ACT = mybir.ActivationFunctionType
F32 = mybir.dt.float32
F32R = mybir.dt.float32r
BF16 = mybir.dt.bfloat16
U8 = mybir.dt.uint8

P = 128
BANKS = 8
EPS = 1e-5
MASKED = -3e38
LEAST_MAX = 1e38
LEAST_SUM = 1e-30

UNSPLIT = ("S", "A", "O", "EO", "F")


class Part:

    def __init__(self, steps, first_step, first_split):
        self.steps = steps
        self.first_step = first_step
        self.first_split = first_split
        self.index = {step: n for n, step in enumerate(steps)}
        self.splits = [sum(s[0] not in UNSPLIT for s in steps[:n + 1]) for n in range(len(steps))]

    def bank(self, step):
        return (self.first_step + self.index[step]) % BANKS

    def done(self, step, i=0):
        return self.first_step + self.index[step] + 1 + i * len(self.steps)

    def split(self, step, i=0):
        return self.first_split + self.splits[self.index[step]] + i * self.splits[-1]

    def fillable(self, step, *operands, i=0):
        n = max([self.index[step] - BANKS + 1] + [self.index[s] + 1 for s in operands])
        return self.first_step + n + i * len(self.steps)


def flamingo_layer(nc, x, ctx_rows, mask, g_xattn, g_ffn, pos_bias, ln_weight, w_q, w_k, w_v, w_out,
                   w_ffn, w_ffn_scale, ffn_bias, out):
    B, L, D = x.shape
    HD = w_q.shape[0]
    H = HD // P
    C = D // P
    PAIRS = H // 2
    LOOPS = PAIRS - 1
    HB = B // 2
    assert L == P and D == 4 * P and HB * P == 512

    def quarters(kind, s):
        return [(kind, s, j) for j in range(B // 2)]

    PROLOGUE = ([("CT", b) for b in range(B)] + [("TK", 0), ("TV", 0), ("TV", 1), ("TQ", 0)]
                + [("K", 0, 0), ("K", 0, 1)] + [("XT", b) for b in range(B)]
                + [("Q", 0, 0), ("Q", 0, 1), ("TQ", 1), ("TK", 1)] + quarters("S", 0))
    BODY = ([("V", j) for j in range(B // 2)]
            + [("Q", 1, 0), ("Q", 1, 1), ("TQ", 0), ("K", 1, 0), ("PT", 0, 0), ("PT", 0, 1),
               ("K", 1, 1), ("TK", 0)] + quarters("A", 0) + quarters("S", 1)
            + [("Q", 0, 0), ("Q", 0, 1), ("TQ", 1), ("K", 0, 0), ("K", 0, 1), ("PT", 1, 0), ("PT", 1, 1),
               ("TK", 1), ("TV", 0), ("TV", 1), ("TO", 0), ("TO", 1)] + quarters("A", 1) + quarters("S", 0)
            + [("O", b) for b in range(B)])
    TAIL = [("O", 0), ("O", 1), ("O", 2), ("O", 3), ("YT", 0), ("O", 4), ("YT", 1), ("F", 0),
            ("O", 5), ("YT", 2), ("F", 1), ("O", 6), ("YT", 3), ("F", 2), ("O", 7), ("YT", 4),
            ("F", 3), ("YT", 5), ("F", 4), ("YT", 6), ("F", 5), ("YT", 7), ("F", 6), ("F", 7)]
    EPILOGUE = ([("V", j) for j in range(B // 2)] + [("TO", 0), ("TO", 1)]
                + [("Q", 1, 0), ("Q", 1, 1), ("K", 1, 0), ("PT", 0, 0), ("PT", 0, 1), ("K", 1, 1)]
                + quarters("A", 0) + quarters("S", 1)
                + [("TF", j) for j in range(C)] + [("EO", b) for b in range(6)]
                + [("PT", 1, 0), ("PT", 1, 1), ("EO", 6), ("EO", 7)]
                + quarters("A", 1) + TAIL)
    assert len(BODY) % BANKS == 0
    pro = Part(PROLOGUE, 0, 0)
    body = Part(BODY, len(PROLOGUE), pro.splits[-1])
    epi = Part(EPILOGUE, len(PROLOGUE) + LOOPS * len(BODY), pro.splits[-1] + LOOPS * body.splits[-1])

    with ExitStack() as stack:
        def sb(name, shape, dtype):
            return stack.enter_context(nc.sbuf_tensor(name, shape, dtype))

        def sem(name):
            return stack.enter_context(nc.semaphore(name))

        banks = [stack.enter_context(nc.psum_tensor(f"bank{k}", [P, 512], F32)) for k in range(BANKS)]

        def halves(name, shape):
            whole = sb(name, [P, 2] + shape[1:], F32R)
            return whole[:, 0], whole[:, 1]

        ctxT = halves("ctxT", [P, C, B * P])
        xT = halves("xT", [P, C, B * P])
        wqT = halves("wqT", [P, C, P])
        wkT = halves("wkT", [P, C, P])
        wvT = halves("wvT", [P, C, 2 * P])
        woT = halves("woT", [P, 2, D])
        qkT_whole = sb("qkT", [P, 2, 2, B * P], F32R)
        qkT = (qkT_whole[:, 0], qkT_whole[:, 1])
        v = halves("v", [P, B, 2 * P])
        pT_whole = sb("pT", [P, 2, B, P], F32R)
        pT = (pT_whole[:, 0], pT_whole[:, 1])
        attnT = halves("attnT", [P, 2, B * P])
        wfT = tuple(t.rearrange("p a (c n) -> p (a c) n", n=D) for t in qkT)

        acc = sb("acc", [P, B, D], F32)
        raw = sb("raw", [P, 8, D], F32)
        scores_area = sb("scores_area", [P, 4, 512], F32)
        rows = sb("rows", [P, 2, D], F32)
        ident = sb("ident", [P, P], F32)
        raw_q = [raw[:, 0, :], raw[:, 1, :]]
        raw_k = [raw[:, 2, :], raw[:, 3, :]]
        raw_v = raw[:, 4:6, :]
        raw_o = raw[:, 6:8, :].rearrange("p a (c n) -> p (a c) n", n=2 * P)
        probs = scores_area[:, 0:2, :].rearrange("p a (b k) -> p (a b) k", k=P)
        biases = scores_area[:, 2:4, :].rearrange("p a (b k) -> p (a b) k", k=P)
        ctx_tile = [scores_area[:, b, :] for b in range(4)] + [raw[:, 6, :], raw[:, 7, :],
                                                               raw[:, 1, :], raw[:, 3, :]]
        x_again = [raw[:, b, :] for b in range(B)]
        out_rows = [raw[:, b, :] for b in range(B)]

        attn_part = sb("attn_part", [P, 2, 2, P], F32)
        attn_sum = sb("attn_sum", [P, 4, 2, P], F32)
        mask_u8 = sb("mask_u8", [P, B, P], U8)
        mask_add = sb("mask_add", [P, B, P], BF16)
        pos = sb("pos", [P, 2, P], F32)
        ln_row = sb("ln_row", [P, D], F32)
        bias_row = sb("bias_row", [P, D], F32)
        scale_col = sb("scale_col", [P, 1], F32)
        gates = sb("gates", [P, 2], F32)
        tanhs = sb("tanhs", [P, 2], F32)
        found_max = sb("found_max", [P, B], F32)
        neg_max = sb("neg_max", [P, B], F32)
        sums = sb("sums", [P, B], F32)
        safe_sums = sb("safe_sums", [P, B], F32)
        recips = sb("recips", [P, B], F32)
        stats = sb("stats", [P, B, 6], F32)
        mean_var = sb("mean_var", [P, B, 2], F32)
        var_eps = sb("var_eps", [P, B], F32)
        std = sb("std", [P, B], F32)
        rstd = sb("rstd", [P, B], F32)
        hvar = sb("hvar", [P, B], F32)
        rms = sb("rms", [P, B], F32)
        rrms = sb("rrms", [P, B], F32)
        shift = sb("shift", [P, B], F32)

        bank_full = sem("bank_full")
        hi_ready = sem("hi_ready")
        evacuated = sem("evacuated")
        ctx_landed = [sem(f"ctx_landed{b}") for b in range(B)]
        x_landed = [sem(f"x_landed{j}") for j in range(B // 2)]
        x_again_landed = [sem(f"x_again_landed{j}") for j in range(3)]
        wq_landed = [sem("wq0_landed"), sem("wq1_landed")]
        wk_landed = [sem("wk0_landed"), sem("wk1_landed")]
        wv_landed = sem("wv_landed")
        wo_landed = sem("wo_landed")
        wf_landed = sem("wf_landed")
        pos_landed = sem("pos_landed")
        mask_landed = sem("mask_landed")
        ln_landed = sem("ln_landed")
        bias_landed = sem("bias_landed")
        scale_landed = sem("scale_landed")
        gates_landed = sem("gates_landed")
        out_landed = sem("out_landed")
        ident_zeroed = sem("ident_zeroed")
        ident_ready = sem("ident_ready")
        mask_ready = sem("mask_ready")
        tanh_ready = sem("tanh_ready")
        bias_ready = sem("bias_ready")
        attn_part_ready = sem("attn_part_ready")
        attn_hi_ready = sem("attn_hi_ready")
        attn_ready = sem("attn_ready")
        score_half_ready = sem("score_half_ready")
        max_found = sem("max_found")
        max_ready = sem("max_ready")
        exps_ready = sem("exps_ready")
        recips_ready = sem("recips_ready")
        probs_ready = sem("probs_ready")
        sums_safe = sem("sums_safe")
        dve_chain = sem("dve_chain")
        var_ready = sem("var_ready")
        std_ready = sem("std_ready")
        ln_rows_ready = sem("ln_rows_ready")
        x_used = sem("x_used")
        wf_scaled = sem("wf_scaled")
        gated_bias_ready = sem("gated_bias_ready")
        norm_ready = sem("norm_ready")
        y_ready = sem("y_ready")
        out_base_ready = sem("out_base_ready")

        wq_heads = w_q.rearrange("(g s p) d -> g s p d", s=2, p=P)
        wk_heads = w_k.rearrange("(g s p) d -> g s p d", s=2, p=P)
        wv_pairs = w_v.rearrange("(g s p) d -> g p s d", s=2, p=P)
        wo_pairs = w_out.rearrange("(c p) (g n) -> g p c n", p=P, n=2 * P)
        pos_pairs = pos_bias.rearrange("(g s) q k -> g q s k", s=2)
        wf_rows = w_ffn.rearrange("(c p) d -> p c d", p=P)

        def target(part, step):
            kind, n = step[0], step[1]
            bank = banks[part.bank(step)][:, :]
            four = bank.rearrange("p (c n) -> p c n", c=C)
            if kind in ("CT", "XT", "YT"):
                dst = xT if kind == "XT" else ctxT
                return [t[:, :, n * P:(n + 1) * P] for t in dst] + [four]
            if kind == "TQ":
                return [t[:, :, :] for t in wqT] + [four]
            if kind == "TK":
                return [t[:, :, :] for t in wkT] + [four]
            if kind == "TV":
                return [t[:, :, n * P:(n + 1) * P] for t in wvT] + [four]
            if kind == "TO":
                return [t[:, n, :] for t in woT] + [bank]
            if kind == "TF":
                return [t[:, :, n * P:(n + 1) * P] for t in wfT] + [four]
            if kind == "V":
                return [t[:, 2 * n:2 * n + 2, :] for t in v] + [bank.rearrange("p (b n) -> p b n", b=2)]
            half = step[2]
            if kind in ("Q", "K"):
                row = 0 if kind == "Q" else 1
                return [t[:, row, half * 512:(half + 1) * 512] for t in qkT] + [bank]
            assert kind == "PT"
            return [t[:, half * HB:(half + 1) * HB, :] for t in pT] + [four]

        def blocks(part, step):
            bank = banks[part.bank(step)][:, :].rearrange("p (b t n) -> p b t n", b=2, t=2)
            return bank[:, :, 0, :], bank[:, :, 1, :]

        def attn_slot(s, j):
            return [t[:, s, 2 * j * P:(2 * j + 2) * P].rearrange("p (b n) -> p b n", b=2) for t in attnT]

        block = stack.enter_context(nc.Block())

        @block.sync
        def _(sp):
            for b in range(B):
                sp.dma_start(ctx_tile[b], ctx_rows[b]).then_inc(ctx_landed[b], 16)
                if b % 2:
                    sp.dma_start(acc[:, b - 1:b + 1, :],
                                 x[b - 1:b + 1].rearrange("b p d -> p b d")).then_inc(x_landed[b // 2], 16)
            sp.dma_start(raw_k[0], wk_heads[0, 0]).then_inc(wk_landed[0], 16)
            sp.dma_start(raw_v, wv_pairs[0]).then_inc(wv_landed, 16)
            sp.dma_start(raw_q[0], wq_heads[0, 0]).then_inc(wq_landed[0], 16)
            sp.wait_ge(bank_full, pro.done(("CT", 7)))
            sp.dma_start(raw_q[1], wq_heads[0, 1]).then_inc(wq_landed[1], 16)
            sp.dma_start(raw_k[1], wk_heads[0, 1]).then_inc(wk_landed[1], 16)
            sp.dma_start(raw_o, wo_pairs[0]).then_inc(wo_landed, 16)
            sp.wait_ge(bank_full, pro.done(("TK", 0)))
            sp.dma_start(raw_k[0], wk_heads[1, 0]).then_inc(wk_landed[0], 16)
            sp.wait_ge(bank_full, pro.done(("TV", 1)))
            sp.dma_start(raw_v, wv_pairs[1]).then_inc(wv_landed, 16)
            sp.wait_ge(bank_full, pro.done(("TQ", 0)))
            sp.dma_start(raw_q[0], wq_heads[1, 0]).then_inc(wq_landed[0], 16)
            sp.wait_ge(bank_full, pro.done(("TQ", 1)))
            sp.dma_start(raw_q[1], wq_heads[1, 1]).then_inc(wq_landed[1], 16)
            sp.wait_ge(bank_full, pro.done(("TK", 1)))
            sp.dma_start(raw_k[1], wk_heads[1, 1]).then_inc(wk_landed[1], 16)

            with sp.Fori(0, LOOPS - 1) as i:
                sp.wait_ge(bank_full, body.done(("TQ", 0), i))
                sp.dma_start(raw_q[0], wq_heads[i + 2, 0]).then_inc(wq_landed[0], 16)
                sp.wait_ge(bias_ready, 2 * i + 2)
                sp.dma_start(pos[:, :, :], pos_pairs[i + 1]).then_inc(pos_landed, 16)
                sp.wait_ge(bank_full, body.done(("TK", 0), i))
                sp.dma_start(raw_k[0], wk_heads[i + 2, 0]).then_inc(wk_landed[0], 16)
                sp.wait_ge(bank_full, body.done(("TQ", 1), i))
                sp.dma_start(raw_q[1], wq_heads[i + 2, 1]).then_inc(wq_landed[1], 16)
                sp.wait_ge(bank_full, body.done(("TK", 1), i))
                sp.dma_start(raw_k[1], wk_heads[i + 2, 1]).then_inc(wk_landed[1], 16)
                sp.wait_ge(bank_full, body.done(("TV", 1), i))
                sp.dma_start(raw_v, wv_pairs[i + 2]).then_inc(wv_landed, 16)
                sp.wait_ge(bank_full, body.done(("TO", 1), i))
                sp.dma_start(raw_o, wo_pairs[i + 1]).then_inc(wo_landed, 16)

            last = LOOPS - 1
            sp.wait_ge(bias_ready, H - 2)
            sp.dma_start(pos[:, :, :], pos_pairs[PAIRS - 1]).then_inc(pos_landed, 16)
            sp.wait_ge(bank_full, body.done(("TK", 1), last))
            sp.dma_start(raw[:, 0:4, :], x[0:4].rearrange("b p d -> p b d")).then_inc(x_again_landed[0], 16)
            sp.wait_ge(bank_full, body.done(("TV", 1), last))
            sp.dma_start(raw[:, 4:6, :], x[4:6].rearrange("b p d -> p b d")).then_inc(x_again_landed[1], 16)
            sp.wait_ge(bank_full, body.done(("TO", 1), last))
            sp.dma_start(raw_o, wo_pairs[PAIRS - 1]).then_inc(wo_landed, 16)
            sp.wait_ge(bank_full, epi.done(("TO", 1)))
            sp.dma_start(raw[:, 6:8, :], x[6:8].rearrange("b p d -> p b d")).then_inc(x_again_landed[2], 16)
            sp.wait_ge(x_used, 4)
            sp.dma_start(raw[:, 0:4, :], wf_rows).then_inc(wf_landed, 16)
            for b in range(B):
                sp.wait_ge(evacuated, epi.done(("F", b)))
                sp.dma_start(out[b], out_rows[b]).then_inc(out_landed, 16)
            sp.wait_ge(out_landed, 16 * B)

        @block.gpsimd
        def _(pool):
            nc.gpsimd.memset(ident[:, :], 0.0).then_inc(ident_zeroed, 1)
            pool.wait_ge(ident_zeroed, 1)
            nc.gpsimd.affine_select(out=ident[:, :], in_=ident[:, :], compare_op=ALU.not_equal, fill=1.0,
                                    base=0, pattern=[[-1, P]], channel_multiplier=1).then_inc(ident_ready, 1)

            def add_bias_and_mask(s, landed, scores_read):
                pool.wait_ge(pos_landed, landed)
                pool.wait_ge(evacuated, scores_read)
                nc.gpsimd.tensor_tensor(biases, mask_add[:, :, :],
                                        pos[:, s, :].unsqueeze(1).to_broadcast([P, B, P]),
                                        ALU.add).then_inc(bias_ready, 1)

            def normalize_probs(head):
                for half in range(2):
                    pool.wait_ge(recips_ready, 2 * head + half + 1)
                    part = probs[:, half * HB:(half + 1) * HB, :]
                    factor = recips[:, half * HB:(half + 1) * HB].unsqueeze(2).to_broadcast([P, HB, P])
                    nc.gpsimd.tensor_tensor(part, part, factor, ALU.mult).then_inc(probs_ready, 1)

            def attention_lo(head, s):
                for j in range(B // 2):
                    hi, lo = attn_slot(s, j)
                    pool.wait_ge(attn_hi_ready, 4 * head + j + 1)
                    nc.gpsimd.tensor_tensor(lo, attn_sum[:, j, :, :], hi.bitcast(F32),
                                            ALU.subtract).then_inc(attn_ready, 1)

            pool.wait_ge(mask_ready, 1)
            pool.wait_ge(bank_full, pro.done(("CT", 7)))
            add_bias_and_mask(0, 16, pro.done(("CT", 0)))
            pool.wait_ge(tanh_ready, 1)
            pool.wait_ge(bias_landed, 16)
            nc.gpsimd.tensor_tensor(bias_row[:, :], bias_row[:, :],
                                    tanhs[:, 1:2].to_broadcast([P, D]), ALU.mult).then_inc(gated_bias_ready, 1)

            with pool.Fori(0, LOOPS) as i:
                normalize_probs(2 * i)
                add_bias_and_mask(1, 16 * i + 16, body.first_step + i * len(BODY))
                attention_lo(2 * i, 0)
                normalize_probs(2 * i + 1)
                add_bias_and_mask(0, 16 * i + 32, body.done(("S", 1, 3), i))
                attention_lo(2 * i + 1, 1)
            normalize_probs(H - 2)
            add_bias_and_mask(1, 16 * PAIRS, epi.first_step)
            attention_lo(H - 2, 0)
            pool.wait_ge(scale_landed, 16)
            pool.wait_ge(wf_landed, 16)
            nc.gpsimd.tensor_tensor(raw[:, 0:4, :], raw[:, 0:4, :],
                                    scale_col[:, 0:1].unsqueeze(2).to_broadcast([P, 4, D]),
                                    ALU.mult).then_inc(wf_scaled, 1)
            normalize_probs(H - 1)
            attention_lo(H - 1, 1)
            pool.wait_ge(gated_bias_ready, 1)
            for b in range(B):
                pool.wait_ge(evacuated, epi.done(("O", b)))
                nc.gpsimd.tensor_tensor(out_rows[b], acc[:, b, :], bias_row[:, :],
                                        ALU.add).then_inc(out_base_ready, 1)

        @block.scalar
        def _(act):
            act.dma_start(mask_u8[:, :, :], mask.rearrange("b q k -> q b k")).then_inc(mask_landed, 16)
            act.dma_start(pos[:, :, :], pos_pairs[0]).then_inc(pos_landed, 16)
            act.dma_start(ln_row[:, :], ln_weight.partition_broadcast(P)).then_inc(ln_landed, 16)
            act.dma_start(gates[:, 0:1], g_xattn.partition_broadcast(P)).then_inc(gates_landed, 16)
            act.dma_start(gates[:, 1:2], g_ffn.partition_broadcast(P)).then_inc(gates_landed, 16)
            act.dma_start(bias_row[:, :], ffn_bias.partition_broadcast(P)).then_inc(bias_landed, 16)
            act.dma_start(scale_col[:, :], w_ffn_scale.partition_broadcast(P)).then_inc(scale_landed, 16)

            def split_hi(part, step, i=0):
                hi, _, bank = target(part, step)
                act.wait_ge(bank_full, part.done(step, i))
                nc.scalar.activation(hi, bank, ACT.Copy).then_inc(hi_ready, 1)

            def attention_part(part, s, j, i):
                step = ("A", s, j)
                if j >= 2:
                    act.wait_ge(evacuated, part.done(("A", s, j - 2), i))
                act.wait_ge(bank_full, part.done(step, i))
                nc.scalar.activation(attn_part[:, j % 2, :, :], blocks(part, step)[1],
                                     ACT.Copy).then_inc(attn_part_ready, 1)

            def attention_hi(part, s, j, i):
                act.wait_ge(evacuated, part.done(("A", s, j), i))
                nc.scalar.activation(attn_slot(s, j)[0], attn_sum[:, j, :, :],
                                     ACT.Copy).then_inc(attn_hi_ready, 1)

            def attention(part, s, i):
                attention_part(part, s, 0, i)
                for j in range(1, B // 2):
                    attention_part(part, s, j, i)
                    attention_hi(part, s, j - 1, i)
                attention_hi(part, s, B // 2 - 1, i)

            def exps(head):
                act.wait_ge(max_ready, head + 1)
                for half in range(2):
                    for b in range(half * HB, (half + 1) * HB):
                        last = nc.scalar.activation(probs[:, b, :], probs[:, b, :], ACT.Exp,
                                                    bias=neg_max[:, b:b + 1], accum_out=sums[:, b:b + 1])
                    last.then_inc(exps_ready, 1)

            for b in range(B):
                split_hi(pro, ("CT", b))
            act.wait_ge(var_ready, 1)
            nc.scalar.activation(std[:, :], var_eps[:, :], ACT.Sqrt).then_inc(std_ready, 1)
            act.wait_ge(var_ready, 2)
            nc.scalar.activation(rms[:, :], hvar[:, :], ACT.Sqrt).then_inc(std_ready, 1)
            act.wait_ge(gates_landed, 32)
            nc.scalar.activation(tanhs[:, :], gates[:, :], ACT.Tanh).then_inc(tanh_ready, 1)
            for step in PROLOGUE[B:]:
                if step[0] not in UNSPLIT:
                    split_hi(pro, step)
            exps(0)

            with act.Fori(0, LOOPS) as i:
                for step in BODY:
                    if step[0] not in UNSPLIT:
                        split_hi(body, step, i)
                    if step == ("A", 0, 0):
                        attention(body, 0, i)
                    if step == ("S", 1, 3):
                        exps(2 * i + 1)
                    if step == ("A", 1, 0):
                        attention(body, 1, i)
                    if step == ("S", 0, 3):
                        exps(2 * i + 2)

            for step in EPILOGUE[:-len(TAIL)]:
                if step[0] not in UNSPLIT:
                    split_hi(epi, step)
                if step == ("A", 0, 0):
                    attention(epi, 0, 0)
                if step == ("S", 1, 3):
                    exps(H - 1)
                if step == ("A", 1, 0):
                    attention(epi, 1, 0)

            def tail_std(b):
                act.wait_ge(var_ready, 3 + b)
                nc.scalar.activation(std[:, b:b + 1], var_eps[:, b:b + 1], ACT.Sqrt).then_inc(std_ready, 1)

            def tail_rows(b):
                act.wait_ge(norm_ready, b + 1)
                nc.scalar.activation(rows[:, b % 2, :], acc[:, b, :], ACT.Identity,
                                     scale=rstd[:, b:b + 1], bias=shift[:, b:b + 1]).then_inc(y_ready, 1)

            for b in range(4):
                tail_std(b)
                if 1 <= b <= 2:
                    tail_rows(b - 1)
            for b in range(B):
                split_hi(epi, ("YT", b))
                if b + 2 < B:
                    tail_rows(b + 2)
                if b + 4 < B:
                    tail_std(b + 4)

        @block.tensor
        def _(pe):
            def transpose_chunks(bank, tile_of, n=C):
                for c in range(n):
                    last = nc.tensor.transpose(bank[:, c * P:(c + 1) * P], tile_of(c), ident[:, :])
                return last

            def products(bank, pairs):
                n = 3 * len(pairs)
                m = 0
                for stationary, moving in pairs:
                    for s, t in ((0, 0), (0, 1), (1, 0)):
                        last = nc.tensor.matmul(bank, stationary[s], moving[t], start=(m == 0), stop=(m == n - 1))
                        m += 1
                return last

            def both(pair, pick):
                return [pick(t) for t in pair]

            def transpose_weights(part, step, i, *operands):
                kind, s = step
                source = {"TQ": raw_q[s], "TK": raw_k[s], "TV": raw_v[:, s, :]}.get(kind)
                pe.wait_ge(evacuated, part.fillable(step, *operands, i=i))
                bank = banks[part.bank(step)]
                if kind == "TO":
                    last = transpose_chunks(bank, lambda c: raw_o[:, c, s * P:(s + 1) * P])
                else:
                    last = transpose_chunks(bank, lambda c: source[:, c * P:(c + 1) * P])
                last.then_inc(bank_full, 1)

            def project(part, step, i, *operands):
                kind, _, half = step
                w, rows_T = (wqT, xT) if kind == "Q" else (wkT, ctxT)
                pe.wait_ge(evacuated, part.fillable(step, *operands, i=i))
                products(banks[part.bank(step)][:, :],
                         [(both(w, lambda t: t[:, c, :]),
                           both(rows_T, lambda t: t[:, c, half * 512:(half + 1) * 512]))
                          for c in range(C)]).then_inc(bank_full, 1)

            def values(part, j, i, *operands):
                step = ("V", j)
                pe.wait_ge(evacuated, part.fillable(step, *operands, i=i))
                for b in (2 * j, 2 * j + 1):
                    last = products(banks[part.bank(step)][:, (b % 2) * 2 * P:(b % 2 + 1) * 2 * P],
                                    [(both(ctxT, lambda t: t[:, c, b * P:(b + 1) * P]),
                                      both(wvT, lambda t: t[:, c, :])) for c in range(C)])
                last.then_inc(bank_full, 1)

            def two_pass(bank, stationary, moving):
                nc.tensor.matmul(bank, stationary[0], moving, start=True, stop=False)
                return nc.tensor.matmul(bank, stationary[1], moving, start=False, stop=True)

            def scores(part, s, j, i, *operands):
                step = ("S", s, j)
                pe.wait_ge(evacuated, part.fillable(step, *operands, i=i))
                for b in (2 * j, 2 * j + 1):
                    last = two_pass(banks[part.bank(step)][:, (b % 2) * 2 * P:(b % 2 + 1) * 2 * P],
                                    both(qkT, lambda t: t[:, 0, b * P:(b + 1) * P]),
                                    qkT_whole[:, :, 1, b * P:(b + 1) * P])
                last.then_inc(bank_full, 1)

            def transpose_probs(part, s, half, i, head):
                step = ("PT", s, half)
                pe.wait_ge(evacuated, part.fillable(step, i=i))
                pe.wait_ge(probs_ready, 2 * head + half + 1)
                transpose_chunks(banks[part.bank(step)],
                                 lambda c: probs[:, half * HB + c, :], HB).then_inc(bank_full, 1)

            def attend(part, s, j, i):
                step = ("A", s, j)
                near = [("PT", s, j // 2)] if part.index[step] - part.index[("PT", s, j // 2)] < BANKS else []
                pe.wait_ge(evacuated, part.fillable(step, *near, i=i))
                for b in (2 * j, 2 * j + 1):
                    last = two_pass(banks[part.bank(step)][:, (b % 2) * 2 * P:(b % 2 + 1) * 2 * P],
                                    both(v, lambda t: t[:, b, s * P:(s + 1) * P]),
                                    pT_whole[:, :, b, :])
                last.then_inc(bank_full, 1)

            def project_out(part, step, heads, i, *operands):
                b = step[1]
                pe.wait_ge(evacuated, part.fillable(step, *operands, i=i))
                products(banks[part.bank(step)][:, :],
                         [(both(attnT, lambda t: t[:, s, b * P:(b + 1) * P]),
                           both(woT, lambda t: t[:, s, :])) for s in heads]).then_inc(bank_full, 1)

            pe.wait_ge(ident_ready, 1)
            for b in range(B):
                pe.wait_ge(ctx_landed[b], 16)
                transpose_chunks(banks[pro.bank(("CT", b))],
                                 lambda c: ctx_tile[b][:, c * P:(c + 1) * P]).then_inc(bank_full, 1)
            pe.wait_ge(wk_landed[0], 16)
            transpose_weights(pro, ("TK", 0), 0)
            pe.wait_ge(wv_landed, 16)
            transpose_weights(pro, ("TV", 0), 0)
            transpose_weights(pro, ("TV", 1), 0)
            pe.wait_ge(wq_landed[0], 16)
            transpose_weights(pro, ("TQ", 0), 0)
            project(pro, ("K", 0, 0), 0, ("TK", 0))
            project(pro, ("K", 0, 1), 0, ("TK", 0))
            for b in range(B):
                pe.wait_ge(evacuated, pro.fillable(("XT", b)))
                pe.wait_ge(ln_rows_ready, b + 1)
                transpose_chunks(banks[pro.bank(("XT", b))],
                                 lambda c: rows[:, b % 2, c * P:(c + 1) * P]).then_inc(bank_full, 1)
            project(pro, ("Q", 0, 0), 0, ("XT", 3))
            project(pro, ("Q", 0, 1), 0, ("XT", 7))
            pe.wait_ge(wq_landed[1], 16)
            transpose_weights(pro, ("TQ", 1), 0)
            pe.wait_ge(wk_landed[1], 16)
            transpose_weights(pro, ("TK", 1), 0)
            for j in range(B // 2):
                scores(pro, 0, j, 0, ("Q", 0, j // 2))

            with pe.Fori(0, LOOPS) as i:
                for j in range(B // 2):
                    values(body, j, i)
                project(body, ("Q", 1, 0), i)
                project(body, ("Q", 1, 1), i)
                pe.wait_ge(wq_landed[0], 16 * i + 32)
                transpose_weights(body, ("TQ", 0), i)
                project(body, ("K", 1, 0), i)
                transpose_probs(body, 0, 0, i, 2 * i)
                transpose_probs(body, 0, 1, i, 2 * i)
                project(body, ("K", 1, 1), i)
                pe.wait_ge(wk_landed[0], 16 * i + 32)
                transpose_weights(body, ("TK", 0), i)
                for j in range(B // 2):
                    attend(body, 0, j, i)
                for j in range(B // 2):
                    scores(body, 1, j, i, *([("K", 1, 1)] if j == 2 else []))

                project(body, ("Q", 0, 0), i)
                project(body, ("Q", 0, 1), i)
                pe.wait_ge(wq_landed[1], 16 * i + 32)
                transpose_weights(body, ("TQ", 1), i)
                project(body, ("K", 0, 0), i)
                project(body, ("K", 0, 1), i)
                transpose_probs(body, 1, 0, i, 2 * i + 1)
                transpose_probs(body, 1, 1, i, 2 * i + 1)
                pe.wait_ge(wk_landed[1], 16 * i + 32)
                transpose_weights(body, ("TK", 1), i)
                pe.wait_ge(wv_landed, 16 * i + 32)
                transpose_weights(body, ("TV", 0), i)
                transpose_weights(body, ("TV", 1), i)
                pe.wait_ge(wo_landed, 16 * i + 16)
                transpose_weights(body, ("TO", 0), i)
                transpose_weights(body, ("TO", 1), i)
                for j in range(B // 2):
                    attend(body, 1, j, i)
                for j in range(B // 2):
                    scores(body, 0, j, i)
                for b in range(B):
                    if b % 2 == 0:
                        pe.wait_ge(attn_ready, 4 * (2 * i + 1) + b // 2 + 1)
                    project_out(body, ("O", b), (0, 1), i)

            for j in range(B // 2):
                values(epi, j, 0)
            pe.wait_ge(wo_landed, 16 * PAIRS)
            transpose_weights(epi, ("TO", 0), 0)
            transpose_weights(epi, ("TO", 1), 0)
            project(epi, ("Q", 1, 0), 0)
            project(epi, ("Q", 1, 1), 0)
            project(epi, ("K", 1, 0), 0)
            transpose_probs(epi, 0, 0, 0, H - 2)
            transpose_probs(epi, 0, 1, 0, H - 2)
            project(epi, ("K", 1, 1), 0)
            for j in range(B // 2):
                attend(epi, 0, j, 0)
            for j in range(B // 2):
                scores(epi, 1, j, 0, *([("K", 1, 1)] if j == 2 else []))
            pe.wait_ge(wf_scaled, 1)
            for j in range(C):
                pe.wait_ge(evacuated, epi.fillable(("TF", j)))
                transpose_chunks(banks[epi.bank(("TF", j))],
                                 lambda c: raw[:, j, c * P:(c + 1) * P]).then_inc(bank_full, 1)
            pe.wait_ge(attn_ready, 4 * (H - 1))
            for b in range(6):
                project_out(epi, ("EO", b), (0,), 0)
            transpose_probs(epi, 1, 0, 0, H - 1)
            transpose_probs(epi, 1, 1, 0, H - 1)
            project_out(epi, ("EO", 6), (0,), 0)
            project_out(epi, ("EO", 7), (0,), 0)
            for j in range(B // 2):
                attend(epi, 1, j, 0)
            for kind, b in TAIL:
                step = (kind, b)
                if kind == "O":
                    pe.wait_ge(attn_ready, 4 * (H - 1) + b // 2 + 1)
                    project_out(epi, step, (1,), 0)
                elif kind == "YT":
                    pe.wait_ge(evacuated, epi.fillable(step))
                    pe.wait_ge(y_ready, b + 1)
                    transpose_chunks(banks[epi.bank(step)],
                                     lambda c: rows[:, b % 2, c * P:(c + 1) * P]).then_inc(bank_full, 1)
                else:
                    pe.wait_ge(evacuated, epi.fillable(step, ("YT", b)))
                    products(banks[epi.bank(step)][:, :],
                             [(both(ctxT, lambda t: t[:, c, b * P:(b + 1) * P]),
                               both(wfT, lambda t: t[:, c, :])) for c in range(C)]).then_inc(bank_full, 1)

        @block.vector
        def _(dve):
            links = [0]

            def chained(instruction):
                links[0] += 1
                instruction.then_inc(dve_chain, 1)
                dve.wait_ge(dve_chain, links[0])

            def split_lo(part, step, i=0):
                hi, lo, bank = target(part, step)
                dve.wait_ge(hi_ready, part.split(step, i))
                nc.vector.tensor_tensor(lo, bank, hi.bitcast(F32), ALU.subtract).then_inc(evacuated, 1)

            def finish_scores(part, s, i, head):
                dve.wait_ge(bias_ready, head + 1)

                def add_second(j):
                    dve.wait_ge(bank_full, part.done(("S", s, j), i))
                    nc.vector.tensor_tensor(probs[:, 2 * j:2 * j + 2, :], blocks(part, ("S", s, j))[1],
                                            biases[:, 2 * j:2 * j + 2, :], ALU.add).then_inc(score_half_ready, 1)

                def add_first(j):
                    dve.wait_ge(score_half_ready, 4 * head + j + 1)
                    nc.vector.tensor_tensor(probs[:, 2 * j:2 * j + 2, :], blocks(part, ("S", s, j))[0],
                                            probs[:, 2 * j:2 * j + 2, :], ALU.add).then_inc(evacuated, 1)

                add_second(0)
                for j in range(1, B // 2):
                    add_second(j)
                    add_first(j - 1)
                add_first(B // 2 - 1)
                dve.wait_ge(evacuated, part.done(("S", s, B // 2 - 1), i))
                nc.vector.tensor_reduce(found_max[:, :], probs, mybir.AxisListType.X, ALU.max,
                                        negate=True).then_inc(max_found, 1)
                dve.wait_ge(max_found, head + 1)
                nc.vector.tensor_scalar_min(neg_max[:, :], found_max[:, :], LEAST_MAX).then_inc(max_ready, 1)

            def sum_attention(part, s, i, head):
                for j in range(B // 2):
                    if s == 1:
                        dve.wait_ge(attn_ready, 4 * head - 4 + j + 1)
                    dve.wait_ge(attn_part_ready, 4 * head + j + 1)
                    nc.vector.tensor_tensor(attn_sum[:, j, :, :], blocks(part, ("A", s, j))[0],
                                            attn_part[:, j % 2, :, :], ALU.add).then_inc(evacuated, 1)

            def invert_sums(head, half):
                cols = slice(half * HB, (half + 1) * HB)
                dve.wait_ge(exps_ready, 2 * head + half + 1)
                nc.vector.tensor_scalar_max(safe_sums[:, cols], sums[:, cols], LEAST_SUM).then_inc(sums_safe, 1)
                dve.wait_ge(sums_safe, 2 * head + half + 1)
                nc.vector.reciprocal(recips[:, cols], safe_sums[:, cols]).then_inc(recips_ready, 1)

            def accumulate(part, step, i=0):
                b = step[1]
                dve.wait_ge(bank_full, part.done(step, i))
                dve.wait_ge(evacuated, part.done(step, i) - BANKS)
                nc.vector.tensor_tensor(acc[:, b, :], banks[part.bank(step)][:, :], acc[:, b, :],
                                        ALU.add).then_inc(evacuated, 1)

            for b in range(B):
                split_lo(pro, ("CT", b))
                if b % 2 == 0:
                    dve.wait_ge(x_landed[b // 2], 16)
                nc.vector.bn_stats(stats[:, b, :], acc[:, b, :]).then_inc(dve_chain, 1)
                links[0] += 1
            dve.wait_ge(dve_chain, links[0])
            for b in range(B):
                nc.vector.bn_aggr(mean_var[:, b, :], stats[:, b, :]).then_inc(dve_chain, 1)
                links[0] += 1
            dve.wait_ge(dve_chain, links[0])
            var = mean_var[:, :, 1]
            nc.vector.tensor_scalar_add(var_eps[:, :], var, EPS).then_inc(var_ready, 1)
            dve.wait_ge(std_ready, 1)
            chained(nc.vector.reciprocal(rstd[:, :], std[:, :]))
            chained(nc.vector.tensor_tensor(rms[:, :], var, rstd[:, :], ALU.mult))
            chained(nc.vector.tensor_tensor(hvar[:, :], rms[:, :], rstd[:, :], ALU.mult))
            nc.vector.tensor_scalar_add(hvar[:, :], hvar[:, :], EPS).then_inc(var_ready, 1)
            dve.wait_ge(mask_landed, 16)
            nc.vector.tensor_scalar(mask_add[:, :, :], mask_u8[:, :, :], -MASKED, MASKED,
                                    ALU.mult, ALU.add).then_inc(mask_ready, 1)
            dve.wait_ge(std_ready, 2)
            chained(nc.vector.reciprocal(rrms[:, :], rms[:, :]))
            dve.wait_ge(ln_landed, 16)

            def normalize_x(b):
                chained(nc.vector.tensor_scalar(acc[:, b, :], acc[:, b, :], mean_var[:, b, 0:1],
                                                rstd[:, b:b + 1], ALU.subtract, ALU.mult))
                if b >= 2:
                    dve.wait_ge(bank_full, pro.done(("XT", b - 2)))
                nc.vector.scalar_tensor_tensor(out=rows[:, b % 2, :], in0=acc[:, b, :],
                                               scalar=rrms[:, b:b + 1], in1=ln_row[:, :],
                                               op0=ALU.mult, op1=ALU.mult).then_inc(ln_rows_ready, 1)

            for step in (("TK", 0), ("TV", 0), ("TV", 1), ("TQ", 0)):
                split_lo(pro, step)
            normalize_x(0)
            normalize_x(1)
            split_lo(pro, ("K", 0, 0))
            split_lo(pro, ("K", 0, 1))
            for b in range(B):
                split_lo(pro, ("XT", b))
                if b + 2 < B:
                    normalize_x(b + 2)
            for step in (("Q", 0, 0), ("Q", 0, 1), ("TQ", 1), ("TK", 1)):
                split_lo(pro, step)
            finish_scores(pro, 0, 0, 0)

            with dve.Fori(0, LOOPS) as i:
                for j in range(B // 2):
                    split_lo(body, ("V", j), i)
                invert_sums(2 * i, 0)
                invert_sums(2 * i, 1)
                for step in (("Q", 1, 0), ("Q", 1, 1), ("TQ", 0), ("K", 1, 0),
                             ("PT", 0, 0), ("PT", 0, 1), ("K", 1, 1), ("TK", 0)):
                    split_lo(body, step, i)
                sum_attention(body, 0, i, 2 * i)
                finish_scores(body, 1, i, 2 * i + 1)
                split_lo(body, ("Q", 0, 0), i)
                invert_sums(2 * i + 1, 0)
                split_lo(body, ("Q", 0, 1), i)
                invert_sums(2 * i + 1, 1)
                for step in (("TQ", 1), ("K", 0, 0), ("K", 0, 1), ("PT", 1, 0), ("PT", 1, 1), ("TK", 1),
                             ("TV", 0), ("TV", 1), ("TO", 0), ("TO", 1)):
                    split_lo(body, step, i)
                sum_attention(body, 1, i, 2 * i + 1)
                finish_scores(body, 0, i, 2 * i + 2)
                for b in range(B):
                    accumulate(body, ("O", b), i)

            for j in range(B // 2):
                split_lo(epi, ("V", j))
            invert_sums(H - 2, 0)
            split_lo(epi, ("TO", 0))
            split_lo(epi, ("TO", 1))
            invert_sums(H - 2, 1)

            def start_x1(b):
                nc.vector.scalar_tensor_tensor(out=acc[:, b, :], in0=acc[:, b, :], scalar=tanhs[:, 0:1],
                                               in1=x_again[b], op0=ALU.mult, op1=ALU.add).then_inc(x_used, 1)

            dve.wait_ge(tanh_ready, 1)
            dve.wait_ge(evacuated, epi.done(("TO", 1)))
            dve.wait_ge(x_again_landed[0], 16)
            for b in range(4):
                start_x1(b)
            split_lo(epi, ("Q", 1, 0))
            dve.wait_ge(x_again_landed[1], 16)
            start_x1(4)
            start_x1(5)
            split_lo(epi, ("Q", 1, 1))
            dve.wait_ge(x_again_landed[2], 16)
            start_x1(6)
            start_x1(7)
            for step in (("K", 1, 0), ("PT", 0, 0), ("PT", 0, 1), ("K", 1, 1)):
                split_lo(epi, step)
            sum_attention(epi, 0, 0, H - 2)
            finish_scores(epi, 1, 0, H - 1)
            for j in range(C):
                split_lo(epi, ("TF", j))

            def add_gated(step):
                b = step[1]
                dve.wait_ge(bank_full, epi.done(step))
                if step == ("O", b):
                    dve.wait_ge(evacuated, epi.done(("EO", b)))
                else:
                    dve.wait_ge(x_used, b + 1)
                nc.vector.scalar_tensor_tensor(out=acc[:, b, :], in0=banks[epi.bank(step)][:, :],
                                               scalar=tanhs[:, 0:1], in1=acc[:, b, :],
                                               op0=ALU.mult, op1=ALU.add).then_inc(evacuated, 1)

            for b in range(4):
                add_gated(("EO", b))
            invert_sums(H - 1, 0)
            add_gated(("EO", 4))
            add_gated(("EO", 5))
            invert_sums(H - 1, 1)
            split_lo(epi, ("PT", 1, 0))
            split_lo(epi, ("PT", 1, 1))
            add_gated(("EO", 6))
            add_gated(("EO", 7))
            sum_attention(epi, 1, 0, H - 1)

            def tail_stats(b):
                dve.wait_ge(evacuated, epi.done(("O", b)))
                chained(nc.vector.bn_stats(stats[:, b, :], acc[:, b, :]))
                chained(nc.vector.bn_aggr(mean_var[:, b, :], stats[:, b, :]))
                nc.vector.tensor_scalar_add(var_eps[:, b:b + 1], mean_var[:, b, 1:2], EPS).then_inc(var_ready, 1)

            def tail_norm(b):
                dve.wait_ge(std_ready, 3 + b)
                chained(nc.vector.reciprocal(rstd[:, b:b + 1], std[:, b:b + 1]))
                nc.vector.scalar_tensor_tensor(out=shift[:, b:b + 1], in0=mean_var[:, b, 0:1], scalar=-1.0,
                                               in1=rstd[:, b:b + 1], op0=ALU.mult,
                                               op1=ALU.mult).then_inc(norm_ready, 1)

            for kind, b in TAIL:
                step = (kind, b)
                if kind == "O":
                    add_gated(step)
                    tail_stats(b)
                    if b:
                        tail_norm(b - 1)
                elif kind == "YT":
                    split_lo(epi, step)
                else:
                    if b == 3:
                        tail_norm(7)
                    dve.wait_ge(out_base_ready, b + 1)
                    dve.wait_ge(bank_full, epi.done(step))
                    nc.vector.scalar_tensor_tensor(out=out_rows[b], in0=banks[epi.bank(step)][:, :],
                                                   scalar=tanhs[:, 1:2], in1=out_rows[b],
                                                   op0=ALU.mult, op1=ALU.add).then_inc(evacuated, 1)


_INS = ['x', 'ctx_4096', 'mask_BxSxS2_bk0', 'g_xattn', 'g_ffn', 'L0_xattn_position_bias',
        'L0_xattn_ln_weight', 'L0_xattn_w_q', 'L0_xattn_w_k', 'L0_xattn_w_v', 'L0_xattn_w_out',
        'L0_ffn_weight', 'L0_ffn_weight_scale', 'L0_ffn_bias']


def kernel(**inputs):
    import numpy as _np
    import concourse.bacc as _bacc
    from concourse import mybir as _mybir
    from concourse.bass_utils import run_bass_kernel_spmd as _run

    nc = _bacc.Bacc("TRN2", target_bir_lowering=False, num_devices=1)
    arrays, args = {}, []
    for name in _INS:
        a = _np.ascontiguousarray(inputs[name])
        arrays[f"in_{name}"] = a
        args.append(nc.dram_tensor(f"in_{name}", a.shape, _mybir.dt.from_np(a.dtype), kind="ExternalInput").ap())
    shape = _np.shape(inputs['x'])
    args.append(nc.dram_tensor("out_0", shape, _mybir.dt.float32, kind="ExternalOutput").ap())
    flamingo_layer(nc, *args)
    r = _run(nc, [arrays], core_ids=[0])
    return r.results[0]["out_0"]
```

```python
from contextlib import ExitStack

import concourse.bass as bass
from concourse import mybir

ALU = mybir.AluOpType
ACT = mybir.ActivationFunctionType
F32 = mybir.dt.float32
F32R = mybir.dt.float32r
BF16 = mybir.dt.bfloat16
U8 = mybir.dt.uint8

P = 128
BANKS = 8
EPS = 1e-5
MASKED = -3e38
LEAST_MAX = 1e38
LEAST_SUM = 1e-30

UNSPLIT = ("S", "A", "O", "EO", "F")


class Part:

    def __init__(self, steps, first_step, first_split):
        self.steps = steps
        self.first_step = first_step
        self.first_split = first_split
        self.index = {step: n for n, step in enumerate(steps)}
        self.splits = [sum(s[0] not in UNSPLIT for s in steps[:n + 1]) for n in range(len(steps))]

    def bank(self, step):
        return (self.first_step + self.index[step]) % BANKS

    def done(self, step, i=0):
        return self.first_step + self.index[step] + 1 + i * len(self.steps)

    def split(self, step, i=0):
        return self.first_split + self.splits[self.index[step]] + i * self.splits[-1]

    def fillable(self, step, *operands, i=0):
        n = max([self.index[step] - BANKS + 1] + [self.index[s] + 1 for s in operands])
        return self.first_step + n + i * len(self.steps)


def flamingo_layer(nc, x, ctx_rows, mask, g_xattn, g_ffn, pos_bias, ln_weight, w_q, w_k, w_v, w_out,
                   w_ffn, w_ffn_scale, ffn_bias, out):
    B, L, D = x.shape
    HD = w_q.shape[0]
    H = HD // P
    C = D // P
    PAIRS = H // 2
    LOOPS = PAIRS - 1
    HB = B // 2
    assert L == P and D == 4 * P and HB * P == 512

    def quarters(kind, s):
        return [(kind, s, j) for j in range(B // 2)]

    PROLOGUE = ([("CT", b) for b in range(B)] + [("K", 0, 0), ("K", 0, 1), ("V", 0), ("V", 1), ("V", 2)]
                + [("XT", b) for b in range(B)]
                + [("Q", 0, 0), ("Q", 0, 1)] + quarters("S", 0) + [("V", 3)])
    SECOND_HEAD = [("K", 1, 0), ("Q", 1, 0), ("Q", 1, 1), ("PT", 0, 0), ("PT", 0, 1), ("K", 1, 1)]
    BODY = (SECOND_HEAD + quarters("A", 0) + quarters("S", 1)
            + [("Q", 0, 0), ("Q", 0, 1), ("K", 0, 0), ("PT", 1, 0), ("K", 0, 1), ("PT", 1, 1)]
            + [("A", 1, 0), ("A", 1, 1), ("S", 0, 0), ("S", 0, 1), ("A", 1, 2), ("A", 1, 3),
               ("S", 0, 2), ("S", 0, 3)]
            + [("V", j) for j in range(B // 2)] + [("O", b) for b in range(B)])
    TAIL = [("O", 0), ("O", 1), ("O", 2), ("O", 3), ("O", 4), ("YT", 0), ("O", 5), ("YT", 1), ("F", 0),
            ("O", 6), ("YT", 2), ("F", 1), ("O", 7), ("YT", 3), ("F", 2), ("YT", 4), ("F", 3),
            ("YT", 5), ("F", 4), ("YT", 6), ("F", 5), ("YT", 7), ("F", 6), ("F", 7)]
    EPILOGUE = (SECOND_HEAD + [("TF", j) for j in range(C)]
                + [("S", 1, 0), ("S", 1, 1), ("A", 0, 0), ("A", 0, 1),
                   ("S", 1, 2), ("S", 1, 3), ("A", 0, 2), ("A", 0, 3)]
                + [("EO", 0), ("EO", 1), ("EO", 2), ("EO", 3), ("PT", 1, 0), ("EO", 4), ("EO", 5),
                   ("A", 1, 0), ("A", 1, 1), ("PT", 1, 1), ("EO", 6), ("EO", 7), ("A", 1, 2), ("A", 1, 3)]
                + TAIL)
    PROLOGUE_UNITS = [("TK", 0), ("TV", 0), ("TV", 1), ("TQ", 0), ("TK", 1), ("TQ", 1)]
    BODY_UNITS = [("TV", 0), ("TV", 1), ("TO", 0), ("TO", 1), ("TQ", 0), ("TK", 0), ("TK", 1), ("TQ", 1)]
    EPILOGUE_UNITS = [("TO", 0), ("TO", 1)]
    assert len(BODY) % BANKS == 0
    pro = Part(PROLOGUE, 0, 0)
    body = Part(BODY, len(PROLOGUE), pro.splits[-1])
    epi = Part(EPILOGUE, len(PROLOGUE) + LOOPS * len(BODY), pro.splits[-1] + LOOPS * body.splits[-1])

    pro_units = Part(PROLOGUE_UNITS, 0, 0)
    body_units = Part(BODY_UNITS, len(PROLOGUE_UNITS), 0)
    epi_units = Part(EPILOGUE_UNITS, len(PROLOGUE_UNITS) + LOOPS * len(BODY_UNITS), 0)

    with ExitStack() as stack:
        def sb(name, shape, dtype):
            return stack.enter_context(nc.sbuf_tensor(name, shape, dtype))

        def sem(name):
            return stack.enter_context(nc.semaphore(name))

        banks = [stack.enter_context(nc.psum_tensor(f"bank{k}", [P, 512], F32)) for k in range(BANKS)]

        def halves(name, shape):
            whole = sb(name, [P, 2] + shape[1:], F32R)
            return whole[:, 0], whole[:, 1]

        ctxT = halves("ctxT", [P, C, B * P])
        xT = halves("xT", [P, C, B * P])
        wqT = halves("wqT", [P, C, P])
        wkT = halves("wkT", [P, C, P])
        wvT = halves("wvT", [P, C, 2 * P])
        woT = halves("woT", [P, 2, D])
        qkT_whole = sb("qkT", [P, 2, 2, B * P], F32R)
        qkT = (qkT_whole[:, 0], qkT_whole[:, 1])
        v = halves("v", [P, B, 2 * P])
        pT_whole = sb("pT", [P, 2, B, P], F32R)
        pT = (pT_whole[:, 0], pT_whole[:, 1])
        attnT = halves("attnT", [P, 2, B * P])
        wfT = tuple(t[:, :, 0:D] for t in xT)

        acc = sb("acc", [P, B, D], F32)
        raw = sb("raw", [P, 8, D], F32)
        scores_area = sb("scores_area", [P, 4, 512], F32)
        rows = sb("rows", [P, 2, D], F32)
        ident = sb("ident", [P, P], F32)
        raw_q, raw_k, raw_v = [raw[:, n:n + 2, :].rearrange("p z (y n) -> p (z y) n", n=2 * P)
                               for n in (0, 2, 4)]
        raw_o = raw[:, 6:8, :]
        weight_f32 = sb("weight_f32", [P, 2, C, P], F32)
        probs = scores_area[:, 0:2, :].rearrange("p a (b k) -> p (a b) k", k=P)
        biases = scores_area[:, 2:4, :].rearrange("p a (b k) -> p (a b) k", k=P)
        ctx_tile = [scores_area[:, b, :] for b in range(4)] + [raw[:, n, :] for n in (6, 7, 0, 1)]
        x_again = [raw[:, b, :] for b in range(B)]
        wf_raw = raw[:, 0:4, :]
        out_rows = [raw[:, b, :] for b in range(B)]

        attn_part = sb("attn_part", [P, 2, 2, P], F32)
        attn_sum = sb("attn_sum", [P, 4, 2, P], F32)
        mask_u8 = sb("mask_u8", [P, B, P], U8)
        mask_add = sb("mask_add", [P, B, P], BF16)
        pos = sb("pos", [P, 2, P], F32)
        ln_row = sb("ln_row", [P, D], F32)
        bias_row = sb("bias_row", [P, D], F32)
        scale_col = sb("scale_col", [P, 1], F32)
        gates = sb("gates", [P, 2], F32)
        tanhs = sb("tanhs", [P, 2], F32)
        found_max = sb("found_max", [P, B], F32)
        neg_max = sb("neg_max", [P, B], F32)
        sums = sb("sums", [P, B], F32)
        safe_sums = sb("safe_sums", [P, B], F32)
        recips = sb("recips", [P, B], F32)
        stats = sb("stats", [P, B, 6], F32)
        mean_var = sb("mean_var", [P, B, 2], F32)
        var_eps = sb("var_eps", [P, B], F32)
        std = sb("std", [P, B], F32)
        rstd = sb("rstd", [P, B], F32)
        sqrt_dummy = sb("sqrt_dummy", [P, 1], F32)
        hvar = sb("hvar", [P, B], F32)
        rms = sb("rms", [P, B], F32)
        rrms = sb("rrms", [P, B], F32)
        shift = sb("shift", [P, B], F32)

        bank_full = sem("bank_full")
        hi_ready = sem("hi_ready")
        evacuated = sem("evacuated")
        ctx_landed = [sem(f"ctx_landed{b}") for b in range(B)]
        x_landed = [sem(f"x_landed{j}") for j in range(B // 2)]
        x_again_landed = [sem(f"x_again_landed{j}") for j in range(3)]
        wq_landed = sem("wq_landed")
        wk_landed = sem("wk_landed")
        wv_landed = sem("wv_landed")
        wo_landed = sem("wo_landed")
        wf_landed = [sem(f"wf_landed{h}") for h in range(2)]
        pos_landed = sem("pos_landed")
        mask_landed = sem("mask_landed")
        ln_landed = sem("ln_landed")
        bias_landed = sem("bias_landed")
        scale_landed = sem("scale_landed")
        gates_landed = sem("gates_landed")
        out_landed = sem("out_landed")
        ident_zeroed = sem("ident_zeroed")
        ident_ready = sem("ident_ready")
        mask_ready = sem("mask_ready")
        tanh_ready = sem("tanh_ready")
        bias_ready = sem("bias_ready")
        w_transposed = sem("w_transposed")
        w_hi_ready = sem("w_hi_ready")
        w_ready = sem("w_ready")
        attn_part_ready = sem("attn_part_ready")
        attn_hi_ready = sem("attn_hi_ready")
        attn_ready = sem("attn_ready")
        score_half_ready = sem("score_half_ready")
        max_found = sem("max_found")
        max_ready = sem("max_ready")
        exps_ready = sem("exps_ready")
        recips_ready = sem("recips_ready")
        probs_ready = sem("probs_ready")
        sums_safe = sem("sums_safe")
        dve_chain = sem("dve_chain")
        var_ready = sem("var_ready")
        std_ready = sem("std_ready")
        x_norm_ready = sem("x_norm_ready")
        x_normalized = sem("x_normalized")
        ln_rows_ready = sem("ln_rows_ready")
        x_used = sem("x_used")
        wf_scaled = sem("wf_scaled")
        gated_bias_ready = sem("gated_bias_ready")
        norm_ready = sem("norm_ready")
        y_ready = sem("y_ready")
        out_base_ready = sem("out_base_ready")

        wq_blocks, wk_blocks, wv_blocks = [
            w.rearrange("(h k r) (c g a) -> h g r c k a", k=8, r=32, g=4, a=32) for w in (w_q, w_k, w_v)]
        wo_blocks = w_out.rearrange("(k r) (h s g a) -> h g r s k a", r=32, s=2, g=4, a=32)
        pos_pairs = pos_bias.rearrange("(g s) q k -> g q s k", s=2)
        wf_rows = w_ffn.rearrange("(c p) d -> p c d", p=P)

        def target(part, step):
            kind, n = step[0], step[1]
            bank = banks[part.bank(step)][:, :]
            four = bank.rearrange("p (c n) -> p c n", c=C)
            if kind in ("CT", "XT", "YT"):
                dst = xT if kind == "XT" else ctxT
                return [t[:, :, n * P:(n + 1) * P] for t in dst] + [four]
            if kind == "TF":
                return [t[:, :, n * P:(n + 1) * P] for t in wfT] + [four]
            if kind == "V":
                return [t[:, 2 * n:2 * n + 2, :] for t in v] + [bank.rearrange("p (b n) -> p b n", b=2)]
            half = step[2]
            if kind in ("Q", "K"):
                row = 0 if kind == "Q" else 1
                return [t[:, row, half * 512:(half + 1) * 512] for t in qkT] + [bank]
            assert kind == "PT"
            return [t[:, half * HB:(half + 1) * HB, :] for t in pT] + [four]

        def weight_unit(units, unit):
            kind, s = unit
            flat = weight_f32[:, (units.first_step + units.index[unit]) % 2, :, :]
            if kind == "TO":
                return raw_o[:, s, :].rearrange("p (c n) -> p c n", n=P), flat, *[
                    t[:, s, :].rearrange("p (c n) -> p c n", n=P) for t in woT]
            source = {"TQ": raw_q, "TK": raw_k, "TV": raw_v}[kind][:, :, s * P:(s + 1) * P]
            if kind == "TV":
                return source, flat, *[t[:, :, s * P:(s + 1) * P] for t in wvT]
            return source, flat, *(wqT if kind == "TQ" else wkT)

        def blocks(part, step):
            bank = banks[part.bank(step)][:, :].rearrange("p (b t n) -> p b t n", b=2, t=2)
            return bank[:, :, 0, :], bank[:, :, 1, :]

        def attn_slot(s, j):
            return [t[:, s, 2 * j * P:(2 * j + 2) * P].rearrange("p (b n) -> p b n", b=2) for t in attnT]

        block = stack.enter_context(nc.Block())

        @block.sync
        def _(sp):
            def load_blocks(raw_blocks, source, landed):
                for g in range(4):
                    sp.dma_start(raw_blocks[32 * g:32 * (g + 1)], source(g)).then_inc(landed, 16)

            def load_q(pair):
                load_blocks(raw_q.rearrange("p c (k a) -> p c k a", a=32), lambda g: wq_blocks[pair, g], wq_landed)

            def load_k(pair):
                load_blocks(raw_k.rearrange("p c (k a) -> p c k a", a=32), lambda g: wk_blocks[pair, g], wk_landed)

            def load_v(pair):
                load_blocks(raw_v.rearrange("p c (k a) -> p c k a", a=32), lambda g: wv_blocks[pair, g], wv_landed)

            def load_o(pair):
                for s in range(2):
                    load_blocks(raw_o[:, s, :].rearrange("p (k a) -> p k a", a=32),
                                lambda g: wo_blocks[pair, g, :, s], wo_landed)

            for b in range(B):
                sp.dma_start(ctx_tile[b], ctx_rows[b]).then_inc(ctx_landed[b], 16)
                if b == 3:
                    load_k(0)
            load_v(0)
            for j in range(B // 2):
                sp.dma_start(acc[:, 2 * j:2 * j + 2, :],
                             x[2 * j:2 * j + 2].rearrange("b p d -> p b d")).then_inc(x_landed[j], 16)
            sp.dma_start(ln_row[:, :], ln_weight.partition_broadcast(P)).then_inc(ln_landed, 16)
            sp.wait_ge(bank_full, pro.done(("CT", 7)))
            load_q(0)
            sp.dma_start(mask_u8[:, :, :], mask.rearrange("b q k -> q b k")).then_inc(mask_landed, 16)
            sp.dma_start(pos[:, :, :], pos_pairs[0]).then_inc(pos_landed, 16)
            sp.dma_start(gates[:, 0:1], g_xattn.partition_broadcast(P)).then_inc(gates_landed, 16)
            sp.dma_start(gates[:, 1:2], g_ffn.partition_broadcast(P)).then_inc(gates_landed, 16)
            sp.dma_start(bias_row[:, :], ffn_bias.partition_broadcast(P)).then_inc(bias_landed, 16)
            sp.dma_start(scale_col[:, :], w_ffn_scale.partition_broadcast(P)).then_inc(scale_landed, 16)
            load_o(0)
            sp.wait_ge(w_transposed, pro_units.done(("TV", 1)))
            load_v(1)
            sp.wait_ge(w_transposed, pro_units.done(("TQ", 1)))
            load_q(1)
            load_k(1)

            with sp.Fori(0, LOOPS - 1) as i:
                sp.wait_ge(w_transposed, body_units.done(("TV", 1), i))
                load_v(i + 2)
                sp.wait_ge(w_transposed, body_units.done(("TO", 1), i))
                load_o(i + 1)
                sp.wait_ge(bias_ready, 2 * i + 2)
                sp.dma_start(pos[:, :, :], pos_pairs[i + 1]).then_inc(pos_landed, 16)
                sp.wait_ge(w_transposed, body_units.done(("TK", 1), i))
                load_k(i + 2)
                sp.wait_ge(w_transposed, body_units.done(("TQ", 1), i))
                load_q(i + 2)

            last = LOOPS - 1
            sp.wait_ge(w_transposed, body_units.done(("TV", 1), last))
            sp.dma_start(raw[:, 4:6, :], x[4:6].rearrange("b p d -> p b d")).then_inc(x_again_landed[1], 16)
            sp.wait_ge(w_transposed, body_units.done(("TO", 1), last))
            load_o(PAIRS - 1)
            sp.wait_ge(bias_ready, H - 2)
            sp.dma_start(pos[:, :, :], pos_pairs[PAIRS - 1]).then_inc(pos_landed, 16)
            sp.wait_ge(w_transposed, body_units.done(("TQ", 1), last))
            sp.dma_start(raw[:, 0:4, :], x[0:4].rearrange("b p d -> p b d")).then_inc(x_again_landed[0], 16)
            for h in range(2):
                sp.wait_ge(x_used, 2 * h + 2)
                sp.dma_start(wf_raw[:, 2 * h:2 * h + 2, :], wf_rows[:, 2 * h:2 * h + 2, :]).then_inc(wf_landed[h], 16)
            sp.wait_ge(w_transposed, epi_units.done(("TO", 1)))
            sp.dma_start(raw[:, 6:8, :], x[6:8].rearrange("b p d -> p b d")).then_inc(x_again_landed[2], 16)
            for b in range(B):
                sp.wait_ge(evacuated, epi.done(("F", b)))
                sp.dma_start(out[b], out_rows[b]).then_inc(out_landed, 16)
            sp.wait_ge(out_landed, 16 * B)

        @block.gpsimd
        def _(pool):
            nc.gpsimd.memset(ident[:, :], 0.0).then_inc(ident_zeroed, 1)
            pool.wait_ge(ident_zeroed, 1)
            nc.gpsimd.affine_select(out=ident[:, :], in_=ident[:, :], compare_op=ALU.not_equal, fill=1.0,
                                    base=0, pattern=[[-1, P]], channel_multiplier=1).then_inc(ident_ready, 1)

            def add_bias_and_mask(s, landed, scores_read):
                pool.wait_ge(pos_landed, landed)
                pool.wait_ge(evacuated, scores_read)
                nc.gpsimd.tensor_tensor(biases, mask_add[:, :, :],
                                        pos[:, s, :].unsqueeze(1).to_broadcast([P, B, P]),
                                        ALU.add).then_inc(bias_ready, 1)

            def normalize_probs(head, halves=(0, 1)):
                for half in halves:
                    pool.wait_ge(recips_ready, 2 * head + half + 1)
                    part = probs[:, half * HB:(half + 1) * HB, :]
                    factor = recips[:, half * HB:(half + 1) * HB].unsqueeze(2).to_broadcast([P, HB, P])
                    nc.gpsimd.tensor_tensor(part, part, factor, ALU.mult).then_inc(probs_ready, 1)

            def weight_lo(units, unit, i=0):
                _, flat, hi, lo = weight_unit(units, unit)
                pool.wait_ge(w_hi_ready, units.done(unit, i))
                nc.gpsimd.tensor_tensor(lo, flat, hi.bitcast(F32), ALU.subtract).then_inc(w_ready, 1)

            def attention_lo(head, s, quarters=range(B // 2)):
                for j in quarters:
                    hi, lo = attn_slot(s, j)
                    pool.wait_ge(attn_hi_ready, 4 * head + j + 1)
                    nc.gpsimd.tensor_tensor(lo, attn_sum[:, j, :, :], hi.bitcast(F32),
                                            ALU.subtract).then_inc(attn_ready, 1)

            for unit in (("TK", 0), ("TV", 0), ("TV", 1), ("TQ", 0)):
                weight_lo(pro_units, unit)
            pool.wait_ge(mask_ready, 1)
            pool.wait_ge(bank_full, pro.done(("CT", 7)))
            add_bias_and_mask(0, 16, pro.done(("CT", 0)))

            weight_lo(pro_units, ("TK", 1))
            weight_lo(pro_units, ("TQ", 1))
            normalize_probs(0)

            with pool.Fori(0, LOOPS) as i:
                for unit in (("TV", 0), ("TV", 1), ("TO", 0), ("TO", 1)):
                    weight_lo(body_units, unit, i)
                weight_lo(body_units, ("TQ", 0), i)
                add_bias_and_mask(1, 16 * i + 16, body.first_step + i * len(BODY))
                weight_lo(body_units, ("TK", 0), i)
                attention_lo(2 * i, 0)
                normalize_probs(2 * i + 1)
                add_bias_and_mask(0, 16 * i + 32, body.done(("S", 1, 3), i))
                attention_lo(2 * i + 1, 1)
                normalize_probs(2 * i + 2)
                weight_lo(body_units, ("TK", 1), i)
                weight_lo(body_units, ("TQ", 1), i)
            weight_lo(epi_units, ("TO", 0))
            pool.wait_ge(scale_landed, 16)
            for h in range(2):
                pool.wait_ge(wf_landed[h], 16)
                nc.gpsimd.tensor_tensor(wf_raw[:, 2 * h:2 * h + 2, :], wf_raw[:, 2 * h:2 * h + 2, :],
                                        scale_col[:, 0:1].unsqueeze(2).to_broadcast([P, 2, D]),
                                        ALU.mult).then_inc(wf_scaled, 1)
            weight_lo(epi_units, ("TO", 1))
            add_bias_and_mask(1, 16 * PAIRS, epi.first_step)
            attention_lo(H - 2, 0, [0, 1])
            normalize_probs(H - 1, [0])
            attention_lo(H - 2, 0, [2, 3])
            normalize_probs(H - 1, [1])
            attention_lo(H - 1, 1)
            pool.wait_ge(tanh_ready, 1)
            pool.wait_ge(bias_landed, 16)
            nc.gpsimd.tensor_tensor(bias_row[:, :], bias_row[:, :],
                                    tanhs[:, 1:2].to_broadcast([P, D]), ALU.mult).then_inc(gated_bias_ready, 1)
            pool.wait_ge(gated_bias_ready, 1)
            for b in range(B):
                pool.wait_ge(evacuated, epi.done(("O", b)))
                nc.gpsimd.tensor_tensor(out_rows[b], acc[:, b, :], bias_row[:, :],
                                        ALU.add).then_inc(out_base_ready, 1)

        @block.scalar
        def _(act):
            act.wait_ge(ident_ready, 1)
            nc.scalar.activation(sqrt_dummy[:, :], ident[:, 0:1], ACT.Sqrt)
            def split_hi(part, step, i=0):
                hi, _, bank = target(part, step)
                act.wait_ge(bank_full, part.done(step, i))
                nc.scalar.activation(hi, bank, ACT.Copy).then_inc(hi_ready, 1)

            def weight_hi(units, unit, last_use=None, i=0):
                _, flat, hi, _ = weight_unit(units, unit)
                act.wait_ge(w_transposed, units.done(unit, i))
                if last_use is not None:
                    act.wait_ge(bank_full, last_use)
                nc.scalar.activation(hi, flat, ACT.Copy).then_inc(w_hi_ready, 1)

            def attention_part(part, s, j, i):
                step = ("A", s, j)
                if j >= 2:
                    act.wait_ge(evacuated, part.done(("A", s, j - 2), i))
                act.wait_ge(bank_full, part.done(step, i))
                nc.scalar.activation(attn_part[:, j % 2, :, :], blocks(part, step)[1],
                                     ACT.Copy).then_inc(attn_part_ready, 1)

            def attention_hi(part, s, j, i):
                act.wait_ge(evacuated, part.done(("A", s, j), i))
                nc.scalar.activation(attn_slot(s, j)[0], attn_sum[:, j, :, :],
                                     ACT.Copy).then_inc(attn_hi_ready, 1)

            def attention(part, s, i, between=None):
                attention_part(part, s, 0, i)
                for j in range(1, B // 2):
                    attention_part(part, s, j, i)
                    if j == 1 and between:
                        between()
                    attention_hi(part, s, j - 1, i)
                attention_hi(part, s, B // 2 - 1, i)

            def exps(head, halves=(0, 1)):
                for half in halves:
                    act.wait_ge(max_ready, 2 * head + half + 1)
                    for b in range(half * HB, (half + 1) * HB):
                        last = nc.scalar.activation(probs[:, b, :], probs[:, b, :], ACT.Exp,
                                                    bias=neg_max[:, b:b + 1], accum_out=sums[:, b:b + 1])
                    last.then_inc(exps_ready, 1)

            def normalize_x(b):
                act.wait_ge(x_norm_ready, b // HB + 1)
                nc.scalar.activation(acc[:, b, :], acc[:, b, :], ACT.Identity,
                                     scale=rstd[:, b:b + 1], bias=shift[:, b:b + 1]).then_inc(x_normalized, 1)

            def sqrts(half):
                cols = slice(half * HB, (half + 1) * HB)
                act.wait_ge(var_ready, 2 * half + 1)
                nc.scalar.activation(std[:, cols], var_eps[:, cols], ACT.Sqrt).then_inc(std_ready, 1)
                act.wait_ge(var_ready, 2 * half + 2)
                nc.scalar.activation(rms[:, cols], hvar[:, cols], ACT.Sqrt).then_inc(std_ready, 1)

            for b in range(B):
                split_hi(pro, ("CT", b))
                if b == 3:
                    weight_hi(pro_units, ("TK", 0))
            weight_hi(pro_units, ("TV", 0))
            weight_hi(pro_units, ("TV", 1))
            split_hi(pro, ("K", 0, 0))
            split_hi(pro, ("K", 0, 1))
            sqrts(0)
            split_hi(pro, ("V", 0))
            normalize_x(0)
            normalize_x(1)
            split_hi(pro, ("V", 1))
            sqrts(1)
            normalize_x(2)
            split_hi(pro, ("V", 2))
            normalize_x(3)
            split_hi(pro, ("XT", 0))
            normalize_x(4)
            split_hi(pro, ("XT", 1))
            normalize_x(5)
            split_hi(pro, ("XT", 2))
            normalize_x(6)
            weight_hi(pro_units, ("TQ", 0))
            split_hi(pro, ("XT", 3))
            normalize_x(7)
            for b in range(4, B):
                split_hi(pro, ("XT", b))
            weight_hi(pro_units, ("TK", 1), pro.done(("K", 0, 1)))
            split_hi(pro, ("Q", 0, 0))
            split_hi(pro, ("Q", 0, 1))
            weight_hi(pro_units, ("TQ", 1), pro.done(("Q", 0, 1)))
            act.wait_ge(gates_landed, 32)
            nc.scalar.activation(tanhs[:, :], gates[:, :], ACT.Tanh).then_inc(tanh_ready, 1)
            exps(0)
            split_hi(pro, ("V", 3))

            with act.Fori(0, LOOPS) as i:
                before = body.first_step + i * len(BODY)
                weight_hi(body_units, ("TV", 0), before - B, i)
                weight_hi(body_units, ("TV", 1), before - B, i)
                split_hi(body, ("K", 1, 0), i)
                weight_hi(body_units, ("TO", 0), before, i)
                split_hi(body, ("Q", 1, 0), i)
                weight_hi(body_units, ("TO", 1), before, i)
                for step in (("Q", 1, 1), ("PT", 0, 0), ("PT", 0, 1)):
                    split_hi(body, step, i)
                weight_hi(body_units, ("TQ", 0), body.done(("Q", 1, 1), i), i)
                split_hi(body, ("K", 1, 1), i)
                attention(body, 0, i, lambda: weight_hi(body_units, ("TK", 0), body.done(("K", 1, 1), i), i))
                exps(2 * i + 1)
                for step in (("Q", 0, 0), ("Q", 0, 1), ("K", 0, 0), ("PT", 1, 0), ("K", 0, 1), ("PT", 1, 1)):
                    split_hi(body, step, i)
                attention(body, 1, i)
                exps(2 * i + 2)
                for j in range(3):
                    split_hi(body, ("V", j), i)
                weight_hi(body_units, ("TK", 1), body.done(("K", 0, 1), i), i)
                split_hi(body, ("V", 3), i)
                weight_hi(body_units, ("TQ", 1), body.done(("Q", 0, 1), i), i)

            weight_hi(epi_units, ("TO", 0), epi.first_step)
            split_hi(epi, ("K", 1, 0))
            weight_hi(epi_units, ("TO", 1), epi.first_step)
            for step in (("Q", 1, 0), ("Q", 1, 1), ("PT", 0, 0), ("PT", 0, 1), ("K", 1, 1)):
                split_hi(epi, step)
            for j in range(C):
                split_hi(epi, ("TF", j))
            attention_part(epi, 0, 0, 0)
            attention_part(epi, 0, 1, 0)
            attention_hi(epi, 0, 0, 0)
            attention_hi(epi, 0, 1, 0)
            exps(H - 1, [0])
            attention_part(epi, 0, 2, 0)
            attention_part(epi, 0, 3, 0)
            exps(H - 1, [1])
            attention_hi(epi, 0, 2, 0)
            attention_hi(epi, 0, 3, 0)
            split_hi(epi, ("PT", 1, 0))
            attention_part(epi, 1, 0, 0)
            attention_part(epi, 1, 1, 0)
            split_hi(epi, ("PT", 1, 1))
            attention_hi(epi, 1, 0, 0)
            attention_hi(epi, 1, 1, 0)
            attention_part(epi, 1, 2, 0)
            attention_part(epi, 1, 3, 0)
            attention_hi(epi, 1, 2, 0)
            attention_hi(epi, 1, 3, 0)

            def tail_std(b):
                act.wait_ge(var_ready, 5 + b)
                nc.scalar.activation(std[:, b:b + 1], var_eps[:, b:b + 1], ACT.Sqrt).then_inc(std_ready, 1)

            def tail_rows(b):
                act.wait_ge(norm_ready, b + 1)
                nc.scalar.activation(rows[:, b % 2, :], acc[:, b, :], ACT.Identity,
                                     scale=rstd[:, b:b + 1], bias=shift[:, b:b + 1]).then_inc(y_ready, 1)

            for b in range(2):
                tail_std(b)
                tail_rows(b)
            for b in range(B):
                split_hi(epi, ("YT", b))
                if b + 2 < B:
                    tail_std(b + 2)
                    tail_rows(b + 2)

        @block.tensor
        def _(pe):
            def transpose_chunks(bank, tile_of, n=C):
                for c in range(n):
                    last = nc.tensor.transpose(bank[:, c * P:(c + 1) * P], tile_of(c), ident[:, :])
                return last

            def products(bank, pairs):
                n = 3 * len(pairs)
                m = 0
                for stationary, moving in pairs:
                    for s, t in ((0, 0), (0, 1), (1, 0)):
                        last = nc.tensor.matmul(bank, stationary[s], moving[t], start=(m == 0), stop=(m == n - 1))
                        m += 1
                return last

            def both(pair, pick):
                return [pick(t) for t in pair]

            def project(part, step, i, *operands):
                kind, _, half = step
                w, rows_T = (wqT, xT) if kind == "Q" else (wkT, ctxT)
                pe.wait_ge(evacuated, part.fillable(step, *operands, i=i))
                products(banks[part.bank(step)][:, :],
                         [(both(w, lambda t: t[:, c, :]),
                           both(rows_T, lambda t: t[:, c, half * 512:(half + 1) * 512]))
                          for c in range(C)]).then_inc(bank_full, 1)

            def values(part, j, i, *operands):
                step = ("V", j)
                pe.wait_ge(evacuated, part.fillable(step, *operands, i=i))
                for b in (2 * j, 2 * j + 1):
                    last = products(banks[part.bank(step)][:, (b % 2) * 2 * P:(b % 2 + 1) * 2 * P],
                                    [(both(ctxT, lambda t: t[:, c, b * P:(b + 1) * P]),
                                      both(wvT, lambda t: t[:, c, :])) for c in range(C)])
                last.then_inc(bank_full, 1)

            def two_pass(bank, stationary, moving):
                nc.tensor.matmul(bank, stationary[0], moving, start=True, stop=False)
                return nc.tensor.matmul(bank, stationary[1], moving, start=False, stop=True)

            def scores(part, s, j, i, *operands):
                step = ("S", s, j)
                pe.wait_ge(evacuated, part.fillable(step, *operands, i=i))
                for b in (2 * j, 2 * j + 1):
                    last = two_pass(banks[part.bank(step)][:, (b % 2) * 2 * P:(b % 2 + 1) * 2 * P],
                                    both(qkT, lambda t: t[:, 0, b * P:(b + 1) * P]),
                                    qkT_whole[:, :, 1, b * P:(b + 1) * P])
                last.then_inc(bank_full, 1)

            def transpose_probs(part, s, half, i, head):
                step = ("PT", s, half)
                pe.wait_ge(evacuated, part.fillable(step, i=i))
                pe.wait_ge(probs_ready, 2 * head + half + 1)
                transpose_chunks(banks[part.bank(step)],
                                 lambda c: probs[:, half * HB + c, :], HB).then_inc(bank_full, 1)

            def attend(part, s, j, i):
                step = ("A", s, j)
                near = [("PT", s, j // 2)] if part.index[step] - part.index[("PT", s, j // 2)] < BANKS else []
                pe.wait_ge(evacuated, part.fillable(step, *near, i=i))
                for b in (2 * j, 2 * j + 1):
                    last = two_pass(banks[part.bank(step)][:, (b % 2) * 2 * P:(b % 2 + 1) * 2 * P],
                                    both(v, lambda t: t[:, b, s * P:(s + 1) * P]),
                                    pT_whole[:, :, b, :])
                last.then_inc(bank_full, 1)

            def project_out(part, step, heads, i, *operands):
                b = step[1]
                pe.wait_ge(evacuated, part.fillable(step, *operands, i=i))
                products(banks[part.bank(step)][:, :],
                         [(both(attnT, lambda t: t[:, s, b * P:(b + 1) * P]),
                           both(woT, lambda t: t[:, s, :])) for s in heads]).then_inc(bank_full, 1)

            pe.wait_ge(ident_ready, 1)
            for b in range(B):
                pe.wait_ge(ctx_landed[b], 16)
                transpose_chunks(banks[pro.bank(("CT", b))],
                                 lambda c: ctx_tile[b][:, c * P:(c + 1) * P]).then_inc(bank_full, 1)
            pe.wait_ge(w_ready, pro_units.done(("TK", 0)))
            project(pro, ("K", 0, 0), 0, ("CT", 3))
            project(pro, ("K", 0, 1), 0, ("CT", 7))
            pe.wait_ge(w_ready, pro_units.done(("TV", 1)))

            def transpose_x(b):
                pe.wait_ge(evacuated, pro.fillable(("XT", b)))
                pe.wait_ge(ln_rows_ready, b + 1)
                transpose_chunks(banks[pro.bank(("XT", b))],
                                 lambda c: rows[:, b % 2, c * P:(c + 1) * P]).then_inc(bank_full, 1)

            for step in PROLOGUE[PROLOGUE.index(("V", 0)):PROLOGUE.index(("Q", 0, 0))]:
                if step[0] == "V":
                    values(pro, step[1], 0)
                else:
                    transpose_x(step[1])
            pe.wait_ge(w_ready, pro_units.done(("TQ", 0)))
            project(pro, ("Q", 0, 0), 0, ("XT", 3))
            project(pro, ("Q", 0, 1), 0, ("XT", 7))
            for j in range(B // 2):
                scores(pro, 0, j, 0, ("Q", 0, j // 2))
            values(pro, 3, 0)

            with pe.Fori(0, LOOPS) as i:
                pe.wait_ge(w_ready, body_units.first_step - 1 + i * len(BODY_UNITS))
                project(body, ("K", 1, 0), i)
                pe.wait_ge(w_ready, body_units.first_step + i * len(BODY_UNITS))
                project(body, ("Q", 1, 0), i)
                project(body, ("Q", 1, 1), i)
                transpose_probs(body, 0, 0, i, 2 * i)
                transpose_probs(body, 0, 1, i, 2 * i)
                project(body, ("K", 1, 1), i)
                for j in range(B // 2):
                    attend(body, 0, j, i)
                for j in range(B // 2):
                    scores(body, 1, j, i, *([("K", 1, 1)] if j == 2 else []))

                pe.wait_ge(w_ready, body_units.done(("TQ", 0), i))
                project(body, ("Q", 0, 0), i)
                project(body, ("Q", 0, 1), i)
                pe.wait_ge(w_ready, body_units.done(("TK", 0), i))
                project(body, ("K", 0, 0), i)
                transpose_probs(body, 1, 0, i, 2 * i + 1)
                project(body, ("K", 0, 1), i)
                transpose_probs(body, 1, 1, i, 2 * i + 1)
                attend(body, 1, 0, i)
                attend(body, 1, 1, i)
                scores(body, 0, 0, i, ("K", 0, 0))
                scores(body, 0, 1, i)
                attend(body, 1, 2, i)
                attend(body, 1, 3, i)
                scores(body, 0, 2, i, ("K", 0, 1))
                scores(body, 0, 3, i)
                for j in range(B // 2):
                    values(body, j, i)
                for b in range(B):
                    if b % 2 == 0:
                        pe.wait_ge(attn_ready, 4 * (2 * i + 1) + b // 2 + 1)
                    project_out(body, ("O", b), (0, 1), i)

            pe.wait_ge(w_ready, epi_units.first_step)
            project(epi, ("K", 1, 0), 0)
            project(epi, ("Q", 1, 0), 0)
            project(epi, ("Q", 1, 1), 0)
            transpose_probs(epi, 0, 0, 0, H - 2)
            transpose_probs(epi, 0, 1, 0, H - 2)
            project(epi, ("K", 1, 1), 0)
            for j in range(C):
                pe.wait_ge(wf_scaled, j // 2 + 1)
                pe.wait_ge(evacuated, epi.fillable(("TF", j)))
                transpose_chunks(banks[epi.bank(("TF", j))],
                                 lambda c: wf_raw[:, j, c * P:(c + 1) * P]).then_inc(bank_full, 1)
            for j in (0, 2):
                scores(epi, 1, j, 0, ("K", 1, 1) if j == 2 else ("Q", 1, 0))
                scores(epi, 1, j + 1, 0)
                attend(epi, 0, j, 0)
                attend(epi, 0, j + 1, 0)

            def first_head_out(*batches):
                for b in batches:
                    pe.wait_ge(attn_ready, 4 * (H - 2) + b // 2 + 1)
                    project_out(epi, ("EO", b), (0,), 0)

            pe.wait_ge(w_ready, epi_units.done(("TO", 1)))
            first_head_out(0, 1, 2, 3)
            transpose_probs(epi, 1, 0, 0, H - 1)
            first_head_out(4, 5)
            attend(epi, 1, 0, 0)
            attend(epi, 1, 1, 0)
            transpose_probs(epi, 1, 1, 0, H - 1)
            first_head_out(6, 7)
            attend(epi, 1, 2, 0)
            attend(epi, 1, 3, 0)
            for kind, b in TAIL:
                step = (kind, b)
                if kind == "O":
                    pe.wait_ge(attn_ready, 4 * (H - 1) + b // 2 + 1)
                    project_out(epi, step, (1,), 0)
                elif kind == "YT":
                    pe.wait_ge(evacuated, epi.fillable(step))
                    pe.wait_ge(y_ready, b + 1)
                    transpose_chunks(banks[epi.bank(step)],
                                     lambda c: rows[:, b % 2, c * P:(c + 1) * P]).then_inc(bank_full, 1)
                else:
                    pe.wait_ge(evacuated, epi.fillable(step, ("YT", b)))
                    products(banks[epi.bank(step)][:, :],
                             [(both(ctxT, lambda t: t[:, c, b * P:(b + 1) * P]),
                               both(wfT, lambda t: t[:, c, :])) for c in range(C)]).then_inc(bank_full, 1)

        @block.vector
        def _(dve):
            links = [0]

            def chained(instruction):
                links[0] += 1
                instruction.then_inc(dve_chain, 1)
                dve.wait_ge(dve_chain, links[0])

            def split_lo(part, step, i=0):
                hi, lo, bank = target(part, step)
                dve.wait_ge(hi_ready, part.split(step, i))
                nc.vector.tensor_tensor(lo, bank, hi.bitcast(F32), ALU.subtract).then_inc(evacuated, 1)

            def transpose_weights(units, unit, landed, i=0):
                source, flat, _, _ = weight_unit(units, unit)
                dve.wait_ge({"TQ": wq_landed, "TK": wk_landed, "TV": wv_landed, "TO": wo_landed}[unit[0]], landed)
                if units is not pro_units or units.index[unit] >= 2:
                    dve.wait_ge(w_ready, units.done(unit, i) - 2)
                nc.vector.transpose(flat, source).then_inc(w_transposed, 1)

            def score_steps(part, s, i, head):
                dve.wait_ge(bias_ready, head + 1)

                def add_second(j):
                    dve.wait_ge(bank_full, part.done(("S", s, j), i))
                    nc.vector.tensor_tensor(probs[:, 2 * j:2 * j + 2, :], blocks(part, ("S", s, j))[1],
                                            biases[:, 2 * j:2 * j + 2, :], ALU.add).then_inc(score_half_ready, 1)

                def add_first(j):
                    dve.wait_ge(score_half_ready, 4 * head + j + 1)
                    nc.vector.tensor_tensor(probs[:, 2 * j:2 * j + 2, :], blocks(part, ("S", s, j))[0],
                                            probs[:, 2 * j:2 * j + 2, :], ALU.add).then_inc(evacuated, 1)

                def maximum(half):
                    cols = slice(half * HB, (half + 1) * HB)
                    dve.wait_ge(evacuated, part.done(("S", s, 2 * half + 1), i))
                    nc.vector.tensor_reduce(found_max[:, cols], probs[:, cols, :], mybir.AxisListType.X,
                                            ALU.max, negate=True).then_inc(max_found, 1)
                    dve.wait_ge(max_found, 2 * head + half + 1)
                    nc.vector.tensor_scalar_min(neg_max[:, cols], found_max[:, cols],
                                                LEAST_MAX).then_inc(max_ready, 1)

                def add_half(half):
                    add_second(2 * half)
                    add_second(2 * half + 1)
                    add_first(2 * half)
                    add_first(2 * half + 1)

                return add_half, maximum

            def sum_attention(part, s, j, i, head):
                if s == 1:
                    dve.wait_ge(attn_ready, 4 * head - 4 + j + 1)
                dve.wait_ge(attn_part_ready, 4 * head + j + 1)
                nc.vector.tensor_tensor(attn_sum[:, j, :, :], blocks(part, ("A", s, j))[0],
                                        attn_part[:, j % 2, :, :], ALU.add).then_inc(evacuated, 1)

            def invert_sums(head, half):
                cols = slice(half * HB, (half + 1) * HB)
                dve.wait_ge(exps_ready, 2 * head + half + 1)
                nc.vector.tensor_scalar_max(safe_sums[:, cols], sums[:, cols], LEAST_SUM).then_inc(sums_safe, 1)
                dve.wait_ge(sums_safe, 2 * head + half + 1)
                nc.vector.reciprocal(recips[:, cols], safe_sums[:, cols]).then_inc(recips_ready, 1)

            def accumulate(part, step, i=0):
                b = step[1]
                dve.wait_ge(bank_full, part.done(step, i))
                dve.wait_ge(evacuated, part.done(step, i) - BANKS)
                nc.vector.tensor_tensor(acc[:, b, :], banks[part.bank(step)][:, :], acc[:, b, :],
                                        ALU.add).then_inc(evacuated, 1)

            for b in range(B):
                split_lo(pro, ("CT", b))
                if b == 3:
                    transpose_weights(pro_units, ("TK", 0), 64)
            transpose_weights(pro_units, ("TV", 0), 64)
            transpose_weights(pro_units, ("TV", 1), 64)

            def row_stats(b):
                if b % 2 == 0:
                    dve.wait_ge(x_landed[b // 2], 16)
                nc.vector.bn_stats(stats[:, b, :], acc[:, b, :]).then_inc(dve_chain, 1)
                links[0] += 1

            def variance(half):
                dve.wait_ge(dve_chain, links[0])
                for b in range(half * HB, (half + 1) * HB):
                    nc.vector.bn_aggr(mean_var[:, b, :], stats[:, b, :]).then_inc(dve_chain, 1)
                    links[0] += 1
                dve.wait_ge(dve_chain, links[0])
                cols = slice(half * HB, (half + 1) * HB)
                nc.vector.tensor_scalar_add(var_eps[:, cols], mean_var[:, cols, 1], EPS).then_inc(var_ready, 1)

            def norm_factors(half):
                cols = slice(half * HB, (half + 1) * HB)
                mean, var = mean_var[:, cols, 0], mean_var[:, cols, 1]
                dve.wait_ge(std_ready, 2 * half + 1)
                chained(nc.vector.reciprocal(rstd[:, cols], std[:, cols]))
                nc.vector.scalar_tensor_tensor(out=shift[:, cols], in0=mean, scalar=-1.0, in1=rstd[:, cols],
                                               op0=ALU.mult, op1=ALU.mult).then_inc(x_norm_ready, 1)
                chained(nc.vector.tensor_tensor(rms[:, cols], var, rstd[:, cols], ALU.mult))
                chained(nc.vector.tensor_tensor(hvar[:, cols], rms[:, cols], rstd[:, cols], ALU.mult))
                nc.vector.tensor_scalar_add(hvar[:, cols], hvar[:, cols], EPS).then_inc(var_ready, 1)

            def rms_factors(half):
                cols = slice(half * HB, (half + 1) * HB)
                dve.wait_ge(std_ready, 2 * half + 2)
                chained(nc.vector.reciprocal(rrms[:, cols], rms[:, cols]))

            def weigh_rows(b):
                dve.wait_ge(x_normalized, b + 1)
                if b >= 2:
                    dve.wait_ge(bank_full, pro.done(("XT", b - 2)))
                nc.vector.scalar_tensor_tensor(out=rows[:, b % 2, :], in0=acc[:, b, :],
                                               scalar=rrms[:, b:b + 1], in1=ln_row[:, :],
                                               op0=ALU.mult, op1=ALU.mult).then_inc(ln_rows_ready, 1)

            split_lo(pro, ("K", 0, 0))
            row_stats(0)
            row_stats(1)
            row_stats(2)
            row_stats(3)
            split_lo(pro, ("K", 0, 1))
            variance(0)
            row_stats(4)
            row_stats(5)
            norm_factors(0)
            row_stats(6)
            row_stats(7)
            variance(1)
            rms_factors(0)
            split_lo(pro, ("V", 0))
            norm_factors(1)
            dve.wait_ge(ln_landed, 16)
            weigh_rows(0)
            split_lo(pro, ("V", 1))
            weigh_rows(1)
            rms_factors(1)
            split_lo(pro, ("V", 2))
            split_lo(pro, ("XT", 0))
            weigh_rows(2)
            split_lo(pro, ("XT", 1))
            weigh_rows(3)
            transpose_weights(pro_units, ("TQ", 0), 64)
            split_lo(pro, ("XT", 2))
            weigh_rows(4)
            split_lo(pro, ("XT", 3))
            weigh_rows(5)
            split_lo(pro, ("XT", 4))
            weigh_rows(6)
            split_lo(pro, ("XT", 5))
            weigh_rows(7)
            dve.wait_ge(mask_landed, 16)
            nc.vector.tensor_scalar(mask_add[:, :, :], mask_u8[:, :, :], -MASKED, MASKED,
                                    ALU.mult, ALU.add).then_inc(mask_ready, 1)
            split_lo(pro, ("XT", 6))
            split_lo(pro, ("XT", 7))
            transpose_weights(pro_units, ("TK", 1), 64)
            split_lo(pro, ("Q", 0, 0))
            transpose_weights(pro_units, ("TQ", 1), 64)
            split_lo(pro, ("Q", 0, 1))
            add_half, maximum = score_steps(pro, 0, 0, 0)
            for half in range(2):
                add_half(half)
                maximum(half)
            invert_sums(0, 0)
            invert_sums(0, 1)
            split_lo(pro, ("V", 3))

            with dve.Fori(0, LOOPS) as i:
                transpose_weights(body_units, ("TV", 0), 64 * i + 128, i)
                transpose_weights(body_units, ("TV", 1), 64 * i + 128, i)
                split_lo(body, ("K", 1, 0), i)
                transpose_weights(body_units, ("TO", 0), 128 * i + 128, i)
                split_lo(body, ("Q", 1, 0), i)
                transpose_weights(body_units, ("TO", 1), 128 * i + 128, i)
                for step in (("Q", 1, 1), ("PT", 0, 0), ("PT", 0, 1)):
                    split_lo(body, step, i)
                transpose_weights(body_units, ("TQ", 0), 64 * i + 128, i)
                split_lo(body, ("K", 1, 1), i)
                transpose_weights(body_units, ("TK", 0), 64 * i + 128, i)
                for j in range(B // 2):
                    sum_attention(body, 0, j, i, 2 * i)
                add_half, maximum = score_steps(body, 1, i, 2 * i + 1)
                for half in range(2):
                    add_half(half)
                    maximum(half)
                invert_sums(2 * i + 1, 0)
                invert_sums(2 * i + 1, 1)
                for step in (("Q", 0, 0), ("Q", 0, 1), ("K", 0, 0), ("PT", 1, 0), ("K", 0, 1), ("PT", 1, 1)):
                    split_lo(body, step, i)
                add_half, maximum = score_steps(body, 0, i, 2 * i + 2)
                sum_attention(body, 1, 0, i, 2 * i + 1)
                sum_attention(body, 1, 1, i, 2 * i + 1)
                add_half(0)
                sum_attention(body, 1, 2, i, 2 * i + 1)
                sum_attention(body, 1, 3, i, 2 * i + 1)
                maximum(0)
                add_half(1)
                maximum(1)
                invert_sums(2 * i + 2, 0)
                invert_sums(2 * i + 2, 1)
                for j in range(3):
                    split_lo(body, ("V", j), i)
                transpose_weights(body_units, ("TK", 1), 64 * i + 128, i)
                split_lo(body, ("V", 3), i)
                transpose_weights(body_units, ("TQ", 1), 64 * i + 128, i)
                for b in range(B):
                    accumulate(body, ("O", b), i)

            def start_x1(b):
                nc.vector.scalar_tensor_tensor(out=acc[:, b, :], in0=acc[:, b, :], scalar=tanhs[:, 0:1],
                                               in1=x_again[b], op0=ALU.mult, op1=ALU.add).then_inc(x_used, 1)

            dve.wait_ge(tanh_ready, 1)
            dve.wait_ge(evacuated, epi.first_step)
            dve.wait_ge(x_again_landed[0], 16)
            for b in range(4):
                start_x1(b)
            transpose_weights(epi_units, ("TO", 0), 128 * PAIRS)
            split_lo(epi, ("K", 1, 0))
            transpose_weights(epi_units, ("TO", 1), 128 * PAIRS)
            dve.wait_ge(x_again_landed[1], 16)
            start_x1(4)
            start_x1(5)
            for step in (("Q", 1, 0), ("Q", 1, 1), ("PT", 0, 0), ("PT", 0, 1)):
                split_lo(epi, step)
            dve.wait_ge(x_again_landed[2], 16)
            start_x1(6)
            start_x1(7)
            split_lo(epi, ("K", 1, 1))
            for j in range(C):
                split_lo(epi, ("TF", j))
            add_half, maximum = score_steps(epi, 1, 0, H - 1)
            add_half(0)
            sum_attention(epi, 0, 0, 0, H - 2)
            sum_attention(epi, 0, 1, 0, H - 2)
            maximum(0)
            add_half(1)
            maximum(1)
            invert_sums(H - 1, 0)
            sum_attention(epi, 0, 2, 0, H - 2)
            sum_attention(epi, 0, 3, 0, H - 2)
            invert_sums(H - 1, 1)

            def add_gated(step):
                b = step[1]
                dve.wait_ge(bank_full, epi.done(step))
                if step == ("O", b):
                    dve.wait_ge(evacuated, epi.done(("EO", b)))
                else:
                    dve.wait_ge(x_used, b + 1)
                nc.vector.scalar_tensor_tensor(out=acc[:, b, :], in0=banks[epi.bank(step)][:, :],
                                               scalar=tanhs[:, 0:1], in1=acc[:, b, :],
                                               op0=ALU.mult, op1=ALU.add).then_inc(evacuated, 1)

            for b in range(4):
                add_gated(("EO", b))
            split_lo(epi, ("PT", 1, 0))
            add_gated(("EO", 4))
            add_gated(("EO", 5))
            sum_attention(epi, 1, 0, 0, H - 1)
            sum_attention(epi, 1, 1, 0, H - 1)
            split_lo(epi, ("PT", 1, 1))
            add_gated(("EO", 6))
            add_gated(("EO", 7))
            sum_attention(epi, 1, 2, 0, H - 1)
            sum_attention(epi, 1, 3, 0, H - 1)

            def tail_stats(b):
                dve.wait_ge(evacuated, epi.done(("O", b)))
                chained(nc.vector.bn_stats(stats[:, b, :], acc[:, b, :]))
                chained(nc.vector.bn_aggr(mean_var[:, b, :], stats[:, b, :]))
                nc.vector.tensor_scalar_add(var_eps[:, b:b + 1], mean_var[:, b, 1:2], EPS).then_inc(var_ready, 1)

            def tail_norm(b):
                dve.wait_ge(std_ready, 5 + b)
                chained(nc.vector.reciprocal(rstd[:, b:b + 1], std[:, b:b + 1]))
                nc.vector.scalar_tensor_tensor(out=shift[:, b:b + 1], in0=mean_var[:, b, 0:1], scalar=-1.0,
                                               in1=rstd[:, b:b + 1], op0=ALU.mult,
                                               op1=ALU.mult).then_inc(norm_ready, 1)

            def finish(b):
                step = ("F", b)
                dve.wait_ge(out_base_ready, b + 1)
                dve.wait_ge(bank_full, epi.done(step))
                nc.vector.scalar_tensor_tensor(out=out_rows[b], in0=banks[epi.bank(step)][:, :],
                                               scalar=tanhs[:, 1:2], in1=out_rows[b],
                                               op0=ALU.mult, op1=ALU.add).then_inc(evacuated, 1)

            for step in TAIL:
                if step[0] == "O":
                    add_gated(step)
                elif step[0] == "YT":
                    split_lo(epi, step)
                else:
                    finish(step[1])
                if step in (("O", 0), ("O", 1)):
                    tail_stats(step[1])
                    tail_norm(step[1])
                if step[0] == "YT" and step[1] + 2 < B:
                    tail_stats(step[1] + 2)
                    tail_norm(step[1] + 2)


_INS = ['x', 'ctx_4096', 'mask_BxSxS2_bk0', 'g_xattn', 'g_ffn', 'L0_xattn_position_bias',
        'L0_xattn_ln_weight', 'L0_xattn_w_q', 'L0_xattn_w_k', 'L0_xattn_w_v', 'L0_xattn_w_out',
        'L0_ffn_weight', 'L0_ffn_weight_scale', 'L0_ffn_bias']


def kernel(**inputs):
    import numpy as _np
    import concourse.bacc as _bacc
    from concourse import mybir as _mybir
    from concourse.bass_utils import run_bass_kernel_spmd as _run

    nc = _bacc.Bacc("TRN2", target_bir_lowering=False, num_devices=1)
    arrays, args = {}, []
    for name in _INS:
        a = _np.ascontiguousarray(inputs[name])
        arrays[f"in_{name}"] = a
        args.append(nc.dram_tensor(f"in_{name}", a.shape, _mybir.dt.from_np(a.dtype), kind="ExternalInput").ap())
    shape = _np.shape(inputs['x'])
    args.append(nc.dram_tensor("out_0", shape, _mybir.dt.float32, kind="ExternalOutput").ap())
    flamingo_layer(nc, *args)
    r = _run(nc, [arrays], core_ids=[0])
    return r.results[0]["out_0"]
```
